# Optimizing a Trainium2 kernel written in Bass

```python
import numpy as np
import jax
import jax.numpy as jnp

def _softmax(x, axis=-1):
    return jax.nn.softmax(x, axis=axis)

def _gelu(x):
    return jax.nn.gelu(x, approximate=True)

def _silu(x):
    return jax.nn.silu(x)

def _sigmoid(x):
    return jax.nn.sigmoid(x)

def _layernorm(x, axis=-1, eps=1e-05):
    m = jnp.mean(x, axis=axis, keepdims=True)
    v = jnp.var(x, axis=axis, keepdims=True)
    return (x - m) / jnp.sqrt(v + eps)

def _scatter_add(tgt, idx, src, axis=0):
    return tgt.at[idx].add(src)

def _segment_sum(src, seg, n):
    return jax.ops.segment_sum(src, seg, n)
kernel_name = 'mk_conv_seq_d2_conv_nhwc512_r4_d6e3ec'

def setup_inputs(seed: int=0):
    np.random.seed(seed)
    _w = jnp.asarray

    def _rec_inputs():
        import jax
        import jax.numpy as jnp
        _gk = jax.random.key(seed)
        x = -0.0002928 + 1 * jax.random.normal(jax.random.fold_in(_gk, 1), (8, 32, 32, 128), jnp.float32)
        return x
    x = _rec_inputs()

    def _L0_conv_setup():
        import jax, jax.numpy as jnp
        import numpy as np
        CHANNELS = 128
        NUM_HEADS = 8
        HEAD_DIM = CHANNELS // NUM_HEADS
        EPS = 1e-06
        key = jax.random.key(seed)
        ks = jax.random.split(key, 7)
        c = CHANNELS
        x = jax.random.normal(ks[0], (8, 32, 32, c), dtype=jnp.float32)
        ln_scale = jnp.ones((c,), dtype=jnp.float32)
        ln_bias = jnp.zeros((c,), dtype=jnp.float32)
        w_qkv = jax.random.normal(ks[1], (c, 3 * c), dtype=jnp.float32) / np.sqrt(c)
        b_qkv = jnp.zeros((3 * c,), dtype=jnp.float32)
        w_out = jax.random.normal(ks[2], (c, c), dtype=jnp.float32) / np.sqrt(c)
        b_out = jnp.zeros((c,), dtype=jnp.float32)
        return {'x': x, 'ln_scale': ln_scale, 'ln_bias': ln_bias, 'w_qkv': w_qkv, 'b_qkv': b_qkv, 'w_out': w_out, 'b_out': b_out}
    _L0_conv_all = _L0_conv_setup()
    _L0_conv_in = {k: v for k, v in _L0_conv_all.items() if k in ('ln_scale', 'ln_bias', 'w_qkv', 'b_qkv', 'w_out', 'b_out')}
    del _L0_conv_all

    def _L1_conv_setup():
        import jax, jax.numpy as jnp
        import numpy as np
        NUM_HEADS = 8
        HEAD_DIM = 16
        EMBED = NUM_HEADS * HEAD_DIM
        POOL_H = 4
        POOL_W = 4
        TOP_K = 16
        GH = 32
        GW = 32
        BATCH = 32
        LN_EPS = 0.001

        def _layernorm(x, g, b):
            m = jnp.mean(x, axis=-1, keepdims=True)
            v = jnp.mean(jnp.square(x - m), axis=-1, keepdims=True)
            return (x - m) * jax.lax.rsqrt(v + LN_EPS) * g + b

        def _forward(feature_map, Win, b_in, Wq, Wk, Wv, g1, be1, g2, be2, Wf1, bf1, Wf2, bf2, Wout, bout):
            B, H, W, C = feature_map.shape
            S = H * W
            tokens = feature_map.reshape(B, S, C) @ Win + b_in
            residual = tokens
            t = _layernorm(tokens, g1, be1)

            def heads(x):
                return x.reshape(B, S, NUM_HEADS, HEAD_DIM).transpose(0, 2, 1, 3)
            q = heads(t @ Wq)
            k = heads(t @ Wk)
            v = heads(t @ Wv)

            def pool2d(x):
                oh, ow = (GH // POOL_H, GW // POOL_W)
                xb = x.reshape(B, NUM_HEADS, oh, POOL_H, ow, POOL_W, HEAD_DIM)
                return xb.mean(axis=(3, 5)).reshape(B, NUM_HEADS, oh * ow, HEAD_DIM)
            pk = pool2d(k)
            pv = pool2d(v)
            scores = jnp.einsum('bhsd,bhpd->bhsp', q, pk)
            red = scores.max(axis=(1, 2))
            _, top_idx = jax.lax.top_k(red, TOP_K)
            idx = top_idx[:, None, :, None]
            sel_k = jnp.take_along_axis(pk, idx, axis=2)
            sel_v = jnp.take_along_axis(pv, idx, axis=2)
            scaling = jnp.float32(HEAD_DIM) ** (-0.5)
            attn = jax.nn.softmax(jnp.einsum('bhsd,bhkd->bhsk', q, sel_k) * scaling, axis=-1)
            attn_out = jnp.einsum('bhsk,bhkd->bhsd', attn, sel_v)
            attn_out = attn_out.transpose(0, 2, 1, 3).reshape(B, S, EMBED)
            tokens = residual + attn_out
            residual = tokens
            t2 = _layernorm(tokens, g2, be2)
            ff = jax.nn.gelu(t2 @ Wf1 + bf1, approximate=False) @ Wf2 + bf2
            tokens = residual + ff
            tokens = tokens @ Wout + bout
            return tokens.reshape(B, H, W, C)
        key = jax.random.key(seed)
        ks = jax.random.split(key, 16)
        p = lambda k, shape: jax.random.normal(k, shape, jnp.float32) * 0.02
        return {'feature_map': jax.random.normal(ks[0], (BATCH, GH, GW, EMBED), jnp.float32), 'Win': p(ks[1], (EMBED, EMBED)), 'b_in': jnp.zeros((EMBED,), jnp.float32), 'Wq': p(ks[2], (EMBED, EMBED)), 'Wk': p(ks[3], (EMBED, EMBED)), 'Wv': p(ks[4], (EMBED, EMBED)), 'g1': jnp.ones((EMBED,), jnp.float32), 'be1': jnp.zeros((EMBED,), jnp.float32), 'g2': jnp.ones((EMBED,), jnp.float32), 'be2': jnp.zeros((EMBED,), jnp.float32), 'Wf1': p(ks[5], (EMBED, 2 * EMBED)), 'bf1': jnp.zeros((2 * EMBED,), jnp.float32), 'Wf2': p(ks[6], (2 * EMBED, EMBED)), 'bf2': jnp.zeros((EMBED,), jnp.float32), 'Wout': p(ks[7], (EMBED, EMBED)), 'bout': jnp.zeros((EMBED,), jnp.float32)}
    _L1_conv_all = _L1_conv_setup()
    _L1_conv_in = {k: v for k, v in _L1_conv_all.items() if k in ('Win', 'b_in', 'Wq', 'Wk', 'Wv', 'g1', 'be1', 'g2', 'be2', 'Wf1', 'bf1', 'Wf2', 'bf2', 'Wout', 'bout')}
    del _L1_conv_all
    return {'x': x, 'L0_conv_ln_scale': _L0_conv_in['ln_scale'], 'L0_conv_ln_bias': _L0_conv_in['ln_bias'], 'L0_conv_w_qkv': _L0_conv_in['w_qkv'], 'L0_conv_b_qkv': _L0_conv_in['b_qkv'], 'L0_conv_w_out': _L0_conv_in['w_out'], 'L0_conv_b_out': _L0_conv_in['b_out'], 'L1_conv_Win': _L1_conv_in['Win'], 'L1_conv_b_in': _L1_conv_in['b_in'], 'L1_conv_Wq': _L1_conv_in['Wq'], 'L1_conv_Wk': _L1_conv_in['Wk'], 'L1_conv_Wv': _L1_conv_in['Wv'], 'L1_conv_g1': _L1_conv_in['g1'], 'L1_conv_be1': _L1_conv_in['be1'], 'L1_conv_g2': _L1_conv_in['g2'], 'L1_conv_be2': _L1_conv_in['be2'], 'L1_conv_Wf1': _L1_conv_in['Wf1'], 'L1_conv_bf1': _L1_conv_in['bf1'], 'L1_conv_Wf2': _L1_conv_in['Wf2'], 'L1_conv_bf2': _L1_conv_in['bf2'], 'L1_conv_Wout': _L1_conv_in['Wout'], 'L1_conv_bout': _L1_conv_in['bout']}

def reference(x, L0_conv_ln_scale, L0_conv_ln_bias, L0_conv_w_qkv, L0_conv_b_qkv, L0_conv_w_out, L0_conv_b_out, L1_conv_Win, L1_conv_b_in, L1_conv_Wq, L1_conv_Wk, L1_conv_Wv, L1_conv_g1, L1_conv_be1, L1_conv_g2, L1_conv_be2, L1_conv_Wf1, L1_conv_bf1, L1_conv_Wf2, L1_conv_bf2, L1_conv_Wout, L1_conv_bout):
    import jax
    import jax.numpy as jnp

    def _L0_conv_ref(x, ln_scale, ln_bias, w_qkv, b_qkv, w_out, b_out):
        import jax, jax.numpy as jnp
        import numpy as np
        CHANNELS = 128
        NUM_HEADS = 8
        HEAD_DIM = CHANNELS // NUM_HEADS
        EPS = 1e-06
        b, h, w, c = x.shape
        n = h * w
        mu = jnp.mean(x, axis=-1, keepdims=True)
        var = jnp.var(x, axis=-1, keepdims=True)
        x_norm = (x - mu) * jax.lax.rsqrt(var + EPS) * ln_scale + ln_bias
        x_flat = x_norm.reshape(b, n, c)
        qkv = x_flat @ w_qkv + b_qkv
        q, k, v = jnp.split(qkv, 3, axis=-1)
        q = q.reshape(b, n, NUM_HEADS, HEAD_DIM)
        k = k.reshape(b, n, NUM_HEADS, HEAD_DIM)
        v = v.reshape(b, n, NUM_HEADS, HEAD_DIM)
        scale = HEAD_DIM ** (-0.5)
        attn = jnp.einsum('bqhd,bkhd->bhqk', q, k) * scale
        attn = jax.nn.softmax(attn, axis=-1)
        out = jnp.einsum('bhqk,bkhd->bqhd', attn, v).reshape(b, n, c)
        out = out @ w_out + b_out
        return x + out.reshape(b, h, w, c)

    def _L1_conv_ref(feature_map, Win, b_in, Wq, Wk, Wv, g1, be1, g2, be2, Wf1, bf1, Wf2, bf2, Wout, bout):
        import jax, jax.numpy as jnp
        import numpy as np
        NUM_HEADS = 8
        HEAD_DIM = 16
        EMBED = NUM_HEADS * HEAD_DIM
        POOL_H = 4
        POOL_W = 4
        TOP_K = 16
        GH = 32
        GW = 32
        BATCH = 32
        LN_EPS = 0.001

        def _layernorm(x, g, b):
            m = jnp.mean(x, axis=-1, keepdims=True)
            v = jnp.mean(jnp.square(x - m), axis=-1, keepdims=True)
            return (x - m) * jax.lax.rsqrt(v + LN_EPS) * g + b

        def _forward(feature_map, Win, b_in, Wq, Wk, Wv, g1, be1, g2, be2, Wf1, bf1, Wf2, bf2, Wout, bout):
            B, H, W, C = feature_map.shape
            S = H * W
            tokens = feature_map.reshape(B, S, C) @ Win + b_in
            residual = tokens
            t = _layernorm(tokens, g1, be1)

            def heads(x):
                return x.reshape(B, S, NUM_HEADS, HEAD_DIM).transpose(0, 2, 1, 3)
            q = heads(t @ Wq)
            k = heads(t @ Wk)
            v = heads(t @ Wv)

            def pool2d(x):
                oh, ow = (GH // POOL_H, GW // POOL_W)
                xb = x.reshape(B, NUM_HEADS, oh, POOL_H, ow, POOL_W, HEAD_DIM)
                return xb.mean(axis=(3, 5)).reshape(B, NUM_HEADS, oh * ow, HEAD_DIM)
            pk = pool2d(k)
            pv = pool2d(v)
            scores = jnp.einsum('bhsd,bhpd->bhsp', q, pk)
            red = scores.max(axis=(1, 2))
            _, top_idx = jax.lax.top_k(red, TOP_K)
            idx = top_idx[:, None, :, None]
            sel_k = jnp.take_along_axis(pk, idx, axis=2)
            sel_v = jnp.take_along_axis(pv, idx, axis=2)
            scaling = jnp.float32(HEAD_DIM) ** (-0.5)
            attn = jax.nn.softmax(jnp.einsum('bhsd,bhkd->bhsk', q, sel_k) * scaling, axis=-1)
            attn_out = jnp.einsum('bhsk,bhkd->bhsd', attn, sel_v)
            attn_out = attn_out.transpose(0, 2, 1, 3).reshape(B, S, EMBED)
            tokens = residual + attn_out
            residual = tokens
            t2 = _layernorm(tokens, g2, be2)
            ff = jax.nn.gelu(t2 @ Wf1 + bf1, approximate=False) @ Wf2 + bf2
            tokens = residual + ff
            tokens = tokens @ Wout + bout
            return tokens.reshape(B, H, W, C)
        return _forward(feature_map, Win, b_in, Wq, Wk, Wv, g1, be1, g2, be2, Wf1, bf1, Wf2, bf2, Wout, bout)

    def _gn(v, G=32, eps=1e-05):
        B_, H_, W_, C_ = v.shape
        g = v.reshape(B_, H_, W_, G, C_ // G)
        m = jnp.mean(g, axis=(1, 2, 4), keepdims=True)
        s = jnp.var(g, axis=(1, 2, 4), keepdims=True)
        return ((g - m) / jnp.sqrt(s + eps)).reshape(v.shape)

    def _ln_c(v, eps=1e-06):
        m = jnp.mean(v, axis=-1, keepdims=True)
        s = jnp.var(v, axis=-1, keepdims=True)
        return (v - m) / jnp.sqrt(s + eps)

    def _ln_t(v, eps=1e-05):
        m = jnp.mean(v, axis=-1, keepdims=True)
        s = jnp.var(v, axis=-1, keepdims=True)
        return (v - m) / jnp.sqrt(s + eps)

    def _to_tokens(v):
        B_, H_, W_, C_ = v.shape
        return v.reshape(B_, H_ * W_, C_)

    def _from_tokens(t, like):
        return t.reshape(like.shape)
    x = _L0_conv_ref(x, L0_conv_ln_scale, L0_conv_ln_bias, L0_conv_w_qkv, L0_conv_b_qkv, L0_conv_w_out, L0_conv_b_out)
    x = _L1_conv_ref(x, L1_conv_Win, L1_conv_b_in, L1_conv_Wq, L1_conv_Wk, L1_conv_Wv, L1_conv_g1, L1_conv_be1, L1_conv_g2, L1_conv_be2, L1_conv_Wf1, L1_conv_bf1, L1_conv_Wf2, L1_conv_bf2, L1_conv_Wout, L1_conv_bout)
    return x

_drawn_inputs = setup_inputs


def setup_inputs(seed=0):
    import zlib

    import numpy as np

    out = dict(_drawn_inputs(seed))
    spreads = {'L0_conv_ln_scale': (1.0, 0.6),
     'L0_conv_ln_bias': (0.0, 0.1),
     'L0_conv_b_qkv': (0.0, 0.1),
     'L0_conv_b_out': (0.0, 0.1),
     'L1_conv_b_in': (0.0, 0.1),
     'L1_conv_g1': (1.0, 0.2),
     'L1_conv_be1': (0.0, 0.1),
     'L1_conv_g2': (1.0, 0.6),
     'L1_conv_be2': (0.0, 0.8),
     'L1_conv_bf1': (0.0, 0.272),
     'L1_conv_bf2': (0.0, 0.1),
     'L1_conv_bout': (0.0, 0.1)}
    factors = {'L1_conv_Wq': 19.987}
    for name, (base, spread) in spreads.items():
        noise = np.random.default_rng([zlib.crc32(name.encode()), seed]).standard_normal(out[name].shape)
        drawn = base * np.exp(spread * noise) if base else spread * noise
        out[name] = jnp.asarray(drawn.astype(out[name].dtype))
    for name, factor in factors.items():
        out[name] = (out[name] * factor).astype(out[name].dtype)
    return out
```

```python
import concourse.bass as bass
from concourse import mybir
from contextlib import ExitStack

P = 128
IMAGES, SIDE, C = 8, 32, 128
T = SIDE * SIDE
TILES = T // P
HALF = 512
HEADS, HD = 8, 16
PAIRS = HEADS // 2
PARTS = 3
MROW = PARTS * HD
STEPS = PAIRS * TILES
POOL = 4
GRID = SIDE // POOL
POS = GRID * GRID
TOPK = 16
FF = 2 * C
SCALE = HD ** -0.5
SAFE_SQUARES = 60 / SCALE * 2 / 1.02
LN0_EPS, LN1_EPS = 1e-6, 1e-3
RSQRT_MAGIC = float(0x5F3759DF)

AT_XT, AT_TOKX, AT_XN, AT_Q, AT_K, AT_V, AT_BOUND, AT_FLAG = 4, 5, 9, 11, 12, 14, 16, 18
AT_AT, AT_TOK, AT_T, AT_Q1, AT_PK, AT_SC, AT_RT, AT_RB = 2, 3, 7, 8, 9, 10, 14, 15
AT_SEL, AT_S2, AT_PT, AT_TOK2, AT_TT2, AT_T2, AT_FF, AT_OUT = 17, 18, 21, 22, 23, 26, 27, 30
AT_VA = (15, 18, 26)

BEFORE = 17
AFTER = 38
FIRST_TURNS = BEFORE
TURNS_0 = PAIRS - 1 + BEFORE
TURNS = PAIRS + BEFORE
KQ_TURN = 11
V_TURN = 13
BEFORE_STEPS = 21
AFTER_STEPS = 41


def two_layers(nc, x, ln_scale, ln_bias, w_qkv, b_qkv, w_out, b_out, Win, b_in, Wq, Wk, Wv, g1, be1, g2, be2,
               Wf1, bf1, Wf2, bf2, Wout, bout, out):
    fp32, f32r, bf16, i32 = mybir.dt.float32, mybir.dt.float32r, mybir.dt.bfloat16, mybir.dt.int32
    ALU = mybir.AluOpType
    ACT = mybir.ActivationFunctionType
    AX = mybir.AxisListType

    nc.disable_value_cache = True
    x_v = x.rearrange("n (t a) w c -> n (a w) t c", t=TILES)
    out_v = out.rearrange("n (t a) w c -> n (a w) t c", t=TILES)

    with ExitStack() as ctx:
        def sb(name, shape, dt=fp32):
            return ctx.enter_context(nc.sbuf_tensor(name, shape, dt))

        def sem(name):
            return ctx.enter_context(nc.semaphore(name))

        wqkv_s, wo_s, win_s = sb("wqkv_s", [P, 3 * C]), sb("wo_s", [P, C]), sb("win_s", [P, C])
        wq1_s, wkv1_s, wf1_s = sb("wq1_s", [P, C]), sb("wkv1_s", [P, 2 * C]), sb("wf1_s", [P, FF])
        wf2_s, wout_s = sb("wf2_s", [P, 2, C]), sb("wout_s", [P, C])
        cols = sb("cols", [P, 12])
        LNS, LNB, BQ, BK, G1, BE1, G2, BE2, BF1, BO, BF2 = (cols[:, i:i + 1] for i in (0, 1, 2, 3, 4, 5, 6, 7, 8, 10, 11))
        rows = sb("rows", [P, 3, C])
        wT = sb("wT", [P, 3, C])
        vecB = sb("vecB", [P, 2, C])
        wow = sb("wow", [P, C])
        w2o = sb("w2o", [P, 2, C])
        tok_bias, out_bias = sb("tok_bias", [P, C]), sb("out_bias", [P, C])
        ident = sb("ident", [P, P])
        head_mask = sb("head_mask", [P, HEADS])
        below = sb("below", [POS, POS])
        iota_i, iota_f = sb("iota_i", [POS, TOPK], i32), sb("iota_f", [POS, TOPK])
        ones_row, ones_col = sb("ones_row", [1, POS]), sb("ones_col", [P, 1])
        k_ones = sb("k_ones", [1, T])
        X, xn, xT, xnT = sb("X", [P, TILES, C]), sb("xn", [P, TILES, C]), sb("xT", [P, T]), sb("xnT", [P, T])
        squares, head_mask_b = sb("squares", [P, 2, T], bf16), sb("head_mask_b", [P, HEADS], bf16)
        peak, above, flag = sb("peak", [HEADS, 8]), sb("above", [P, 1]), sb("flag", [1, 1], i32)
        no_maximum = sb("no_maximum", [1, T])
        st0, ln0 = sb("st0", [P, TILES, 6]), sb("ln0", [P, 8, TILES])
        tokx_new, tokx = sb("tokx_new", [P, TILES, C]), sb("tokx", [P, TILES, C])
        qh, ql, kh, kl = (sb(n, [P, T], f32r) for n in ("qh", "ql", "kh", "kl"))
        v_new = sb("v_new", [P, TILES, C])
        Qs = sb("Qs", [P, PAIRS, T], f32r)
        Ks = sb("Ks", [P, HEADS, T], f32r)
        Va = sb("Va", [P, TILES, HEADS, 32])
        Pr = sb("Pr", [P, 2, 2, T])
        mx, mneg = sb("mx", [P, HEADS * TILES]), sb("mneg", [HEADS * TILES, P], f32r)
        Ot, rden = sb("Ot", [P, HALF]), sb("rden", [P, 16])
        attn, attnT = sb("attn", [P, TILES, C]), sb("attnT", [P, T])
        tok, that, tT, q1T = sb("tok", [P, TILES, C]), sb("that", [P, TILES, C]), sb("tT", [P, T]), sb("q1T", [P, T])
        st1, ln1 = sb("st1", [P, TILES, 6]), sb("ln1", [P, 8, TILES])
        pooled, pkT, pkv = sb("pooled", [P, POS]), sb("pkT", [P, POS]), sb("pkv", [POS, 2 * C])
        bd_all = sb("bd_all", [P, HEADS, POS])
        r8, r1, rrow, red = sb("r8", [P, 8]), sb("r1", [P, 1]), sb("rrow", [1, P]), sb("red", [1, POS])
        rB, rsel, rcol = sb("rB", [POS, POS]), sb("rsel", [POS, POS]), sb("rcol", [POS, 1])
        rgt, rank, hot = sb("rgt", [POS, POS]), sb("rank", [POS, 1]), sb("hot", [POS, HEADS, TOPK])
        bd_k, bd_v = sb("bd_k", [P, HEADS, TOPK]), sb("bd_v", [P, HEADS, HD])
        m2, den2 = sb("m2", [P, TILES * HEADS]), sb("den2", [P, TILES * HEADS])
        E2, E2T = sb("E2", [P, TILES * HEADS, TOPK]), sb("E2T", [P, T])
        tok2, tok2T = sb("tok2", [P, TILES, C]), sb("tok2T", [P, T])
        hT, Y = sb("hT", [P, 2, T]), sb("Y", [P, TILES, C])

        S = ctx.enter_context(nc.psum_tensor("S", [P, 2, T], fp32))
        O = ctx.enter_context(nc.psum_tensor("O", [P, HALF], fp32))
        A = ctx.enter_context(nc.psum_tensor("A", [P, HALF], fp32))
        BC = [ctx.enter_context(nc.psum_tensor(f"BC{i}", [P, HALF], fp32)) for i in range(2)]

        weights_in = sem("weights_in")
        consts = sem("consts")
        vsetup = sem("vsetup")
        setup_filled = sem("setup_filled")
        x_in = sem("x_in")
        a_filled, a_drained = sem("a_filled"), sem("a_drained")
        b_filled = [sem("b_filled"), sem("c_filled")]
        b_drained = [sem("b_drained"), sem("c_drained")]
        ln0_ready, xn_ready, ln1_ready, that_ready = sem("ln0_ready"), sem("xn_ready"), sem("ln1_ready"), sem("that_ready")
        before_done = sem("before_done")
        att_done = sem("att_done")
        after_done = sem("after_done")
        squares_ready = sem("squares_ready")
        tokx_moved = sem("tokx_moved")
        va_ready = sem("va_ready")
        stack_in = [sem(f"stack_in{j}") for j in range(PAIRS)]
        mrow_in = sem("mrow_in")
        max_filled, max_drained, mneg_ready, max_turned = sem("max_filled"), sem("max_drained"), sem("mneg_ready"), sem("max_turned")
        scores_ready, probs_ready, pv_done, o_copied = sem("scores_ready"), sem("probs_ready"), sem("pv_done"), sem("o_copied")
        e2_exp, e2_ready = sem("e2_exp"), sem("e2_ready")
        pooled_ready, hot_ready = sem("pooled_ready"), sem("hot_ready")
        out_done = sem("out_done")
        sp_passed, pool_passed, pe_passed, dve_passed = sem("sp_passed"), sem("pool_passed"), sem("pe_passed"), sem("dve_passed")

        STACK_DMAS = 2 * (2 * PARTS + 1)
        MAX_TILES = HEADS * TILES
        WEIGHT_DMAS = 8 + 12 + 3

        def next_turn(turns):
            turns[1] += 1
            return turns[0] + turns[1]

        def half(t, h):
            return t[:, h * HALF:(h + 1) * HALF]

        def tiles4(t, h):
            return t[:, 4 * h:4 * h + 4, :]

        def flat4(t, h):
            return tiles4(t, h).rearrange("p a c -> p (a c)")

        block = ctx.enter_context(nc.Block())

        @block.sync
        def _(sp):
            def load_x(n):
                if not (isinstance(n, int) and n == 0):
                    sp.wait_ge(xn_ready, n)
                    sp.wait_ge(before_done, n * BEFORE_STEPS)
                src = x_v[n] if isinstance(n, int) else x_v[bass.ds(n, 1)].rearrange("o p t c -> (o p) t c")
                sp.dma_start(X[:, :, :], src).then_inc(x_in, 16)

            def stack(n, j, turns_before):
                sp.wait_ge(a_drained, turns_before)
                if not (isinstance(n, int) and n == 0):
                    sp.wait_ge(scores_ready, 2 * STEPS * (n - 1) + 2 * TILES * (j + 1))
                for a in range(2):
                    r = HD * (2 * j + a)
                    for part, (q, k) in enumerate(((qh, kh), (qh, kl), (ql, kh))):
                        d = 64 * a + HD * part
                        sp.dma_start(Qs[d:d + HD, j, :].bitcast(fp32), q[r:r + HD, :].bitcast(fp32)).then_inc(stack_in[j], 16)
                        sp.dma_start(Ks[d:d + HD, 2 * j + a, :].bitcast(fp32), k[r:r + HD, :].bitcast(fp32)).then_inc(stack_in[j], 16)
                    d = 64 * a + MROW
                    sp.dma_start(Qs[d:d + 1, j, :].bitcast(fp32), no_maximum[:, :]).then_inc(stack_in[j], 16)

            def row_maximum(n):
                sp.wait_ge(mneg_ready, n + 1)
                for h in range(HEADS):
                    r = 64 * (h % 2) + MROW
                    sp.dma_start(Qs[r:r + 1, h // 2, :].rearrange("o (t q) -> o t q", t=TILES).bitcast(fp32),
                                 mneg[h * TILES:(h + 1) * TILES, :].bitcast(fp32)).then_inc(mrow_in, 16)

            def store(n):
                sp.wait_ge(b_drained[1], (n + 1) * (AFTER // 2))
                dst = out_v[n] if isinstance(n, int) else out_v[bass.ds(n, 1)].rearrange("o p t c -> (o p) t c")
                sp.dma_start(dst, Y[:, :, :]).then_inc(out_done, 16)

            for dst, src in ((wqkv_s[:, :], w_qkv), (wo_s[:, :], w_out), (win_s[:, :], Win), (wq1_s[:, :], Wq),
                             (wkv1_s[:, 0:C], Wk), (wkv1_s[:, C:2 * C], Wv), (wf1_s[:, :], Wf1),
                             (wf2_s[:, :, :], Wf2.rearrange("(a p) c -> p a c", a=2))):
                sp.dma_start(dst, src).then_inc(weights_in, 16)
            sp.dma_start(wout_s[:, :], Wout).then_inc(weights_in, 16)
            load_x(0)
            col = lambda v, s: v[s:s + C].rearrange("(p o) -> p o", o=1)
            for dst, (v, s) in zip((LNS, LNB, BQ, BK, G1, BE1, G2, BE2, cols[:, 8:9], cols[:, 9:10], BO),
                                   ((ln_scale, 0), (ln_bias, 0), (b_qkv, 0), (b_qkv, C), (g1, 0), (be1, 0), (g2, 0),
                                    (be2, 0), (bf1, 0), (bf1, C), (b_out, 0))):
                sp.dma_start(dst, col(v, s)).then_inc(weights_in, 16)
            sp.dma_start(BF2, col(bf2, 0)).then_inc(weights_in, 16)
            for i, (v, s) in enumerate(((b_qkv, 2 * C), (b_in, 0))):
                sp.dma_start(rows[:, i, :], v[s:s + C].partition_broadcast(P)).then_inc(weights_in, 16)
            sp.dma_start(rows[:, 2, :], bout.partition_broadcast(P)).then_inc(weights_in, 16)
            sp.wait_ge(consts, 9)
            sp.wait_ge(vsetup, 1)
            for h in range(HEADS):
                r = 64 * (h % 2) + MROW
                sp.dma_start(Ks[r:r + 1, h, :].bitcast(fp32), k_ones[:, :]).then_inc(stack_in[h // 2], 16)
            for j in range(PAIRS):
                stack(0, j, KQ_TURN - 1)

            def image(n, base, first=False, last=False):
                sp.wait_ge(a_drained, base)
                sp.sem_inc(sp_passed, 1)
                with sp.If(sp.value_load(flag[0:1, 0:1], min_val=0, max_val=HEADS) > 0):
                    row_maximum(n)
                with sp.Else():
                    sp.sem_inc(mrow_in, 16 * HEADS)
                k_turn = base + (0 if first else 1) + KQ_TURN
                if not last:
                    load_x(n + 1)
                    for j in range(PAIRS - 1):
                        stack(n + 1, j, k_turn)
                if not first:
                    store(n - 1)
                if not last:
                    stack(n + 1, PAIRS - 1, k_turn)

            image(0, FIRST_TURNS, first=True)
            with sp.Fori(1, IMAGES - 1) as n:
                image(n, FIRST_TURNS + TURNS_0 + (n - 1) * TURNS)
            image(IMAGES - 1, FIRST_TURNS + TURNS_0 + (IMAGES - 2) * TURNS, last=True)
            store(IMAGES - 1)
            sp.wait_ge(out_done, 16 * IMAGES)

        @block.gpsimd
        def _(pool):
            def wait(signal, value):
                pool.wait_ge(signal, value)
                pool.sem_inc(pool_passed, 1)

            def step(n, ins):
                ins.then_inc(consts, 1)
                pool.wait_ge(consts, n)

            step(1, pool.memset(ident[:, :], 0.0))
            step(2, pool.affine_select(out=ident[:, :], in_=ident[:, :], compare_op=ALU.not_equal, fill=1.0, base=0,
                                       pattern=[[-1, P]], channel_multiplier=1))
            step(3, pool.memset(head_mask[:, :], 1.0))
            step(4, pool.affine_select(out=head_mask[:, :], in_=head_mask[:, :], compare_op=ALU.is_ge, fill=0.0, base=0,
                                       pattern=[[-HD, HEADS]], channel_multiplier=1))
            step(5, pool.affine_select(out=head_mask[:, :], in_=head_mask[:, :], compare_op=ALU.is_ge, fill=0.0,
                                       base=HD - 1, pattern=[[HD, HEADS]], channel_multiplier=-1))
            step(6, pool.memset(below[:, :], 1.0))
            step(7, pool.affine_select(out=below[:, :], in_=below[:, :], compare_op=ALU.is_gt, fill=0.0, base=0,
                                       pattern=[[-1, POS]], channel_multiplier=1))
            step(8, pool.iota(iota_i[:, :], pattern=[[1, TOPK]], base=0, channel_multiplier=0))
            pool.memset(Ks[:, :, :].bitcast(fp32), 0.0)
            step(9, pool.memset(Qs[:, :, :].bitcast(fp32), 0.0))
            step(10, pool.memset(Va[:, :, :, :], 1.0))

            def normalise(dst, src, ln, ready, need, done):
                wait(ready, need)
                for t in range(TILES):
                    ins = pool.tensor_scalar(dst[:, t, :], src[:, t, :], ln[:, 0, t:t + 1], ln[:, 1, t:t + 1],
                                             ALU.subtract, ALU.mult)
                ins.then_inc(done, 1)

            def place_v(n, j, v_turn):
                wait(a_drained, v_turn)
                if not (isinstance(n, int) and n == 0):
                    wait(pv_done, STEPS * (n - 1) + TILES * (j + 1))
                pool.tensor_copy(Va[:, :, 2 * j:2 * j + 2, 0:HD],
                                 v_new[:, :, 2 * HD * j:2 * HD * (j + 1)].rearrange("p t (h d) -> p t h d", h=2))\
                    .then_inc(va_ready, 1)

            def square(n, k_turn):
                wait(a_drained, k_turn)
                for i, part in enumerate((qh, kh)):
                    ins = pool.tensor_tensor(squares[:, i, :], part[:, :].bitcast(fp32), part[:, :].bitcast(fp32), ALU.mult)
                ins.then_inc(squares_ready, 1)

            normalise(xn, X, ln0, ln0_ready, 1, xn_ready)
            square(0, KQ_TURN - 1)
            for j in range(PAIRS):
                place_v(0, j, V_TURN - 1)

            def image(n, base, first=False, last=False):
                v_turn = base + (0 if first else 1) + V_TURN
                if not first:
                    if not (isinstance(n, int) and n == 0):
                        place_v(n, PAIRS - 1, base)
                    wait(b_drained[1], (n - 1) * (AFTER // 2) + 2)
                wait(a_drained, base)
                pool.tensor_copy(tokx[:, :, :], tokx_new[:, :, :]).then_inc(tokx_moved, 1)
                if not last:
                    if not first:
                        normalise(that, tok, ln1, ln1_ready, 2 * (n - 1) + 1, that_ready)
                    normalise(xn, X, ln0, ln0_ready, n + 2, xn_ready)
                    square(n + 1, v_turn - V_TURN + KQ_TURN)
                    place_v(n + 1, 0, v_turn)
                    place_v(n + 1, 1, v_turn)
                    if not first:
                        normalise(that, tok2, ln1, ln1_ready, 2 * (n - 1) + 2, that_ready)
                    place_v(n + 1, 2, v_turn)
                else:
                    normalise(that, tok, ln1, ln1_ready, 2 * (n - 1) + 1, that_ready)
                    normalise(that, tok2, ln1, ln1_ready, 2 * (n - 1) + 2, that_ready)

            image(0, FIRST_TURNS, first=True)
            with pool.Fori(1, IMAGES - 1) as n:
                image(n, FIRST_TURNS + TURNS_0 + (n - 1) * TURNS)
            image(IMAGES - 1, FIRST_TURNS + TURNS_0 + (IMAGES - 2) * TURNS, last=True)
            normalise(that, tok, ln1, ln1_ready, 2 * IMAGES - 1, that_ready)
            normalise(that, tok2, ln1, ln1_ready, 2 * IMAGES, that_ready)

        @block.tensor
        def _(pe):
            def b_turn(n, k):
                b, before = k % 2, n * (AFTER // 2) + k // 2
                if not (isinstance(before, int) and before == 0):
                    pe.wait_ge(b_drained[b], before)
                return BC[b], b_filled[b]

            def b_ready(n, k):
                pe.wait_ge(b_drained[k % 2], n * (AFTER // 2) + k // 2 + 1)

            def a_turn(turns):
                k = next_turn(turns)
                if not (isinstance(k, int) and k == 1):
                    pe.wait_ge(a_drained, k - 1)

            def before_tasks(n, turns, s):
                if s == AT_XT:
                    pe.wait_ge(x_in, 16 * (n + 1))
                    for h in range(2):
                        a_turn(turns)
                        for t in range(4):
                            mm = pe.transpose(A[:, t * P:(t + 1) * P], X[:, 4 * h + t, :], ident[:, :])
                        mm.then_inc(a_filled, 1)
                if s == AT_TOKX:
                    for h in range(2):
                        a_turn(turns)
                        for t in range(4):
                            mm = pe.matmul(A[:, t * P:(t + 1) * P], xT[:, (4 * h + t) * P:(4 * h + t + 1) * P],
                                           win_s[:, :], start=True, stop=True)
                        mm.then_inc(a_filled, 1)
                if s == AT_XN:
                    pe.wait_ge(xn_ready, n + 1)
                    for h in range(2):
                        a_turn(turns)
                        for t in range(4):
                            mm = pe.transpose(A[:, t * P:(t + 1) * P], xn[:, 4 * h + t, :], ident[:, :])
                        mm.then_inc(a_filled, 1)
                if s in (AT_Q, AT_K):
                    c = 0 if s == AT_Q else C
                    for h in range(2):
                        a_turn(turns)
                        pe.matmul(A[:, :], wqkv_s[:, c:c + C], half(xnT, h), start=True, stop=True).then_inc(a_filled, 1)
                if s == AT_V:
                    for h in range(2):
                        a_turn(turns)
                        for t in range(4):
                            mm = pe.matmul(A[:, t * P:(t + 1) * P], xnT[:, (4 * h + t) * P:(4 * h + t + 1) * P],
                                           wqkv_s[:, 2 * C:3 * C], start=True, stop=True)
                        mm.then_inc(a_filled, 1)

                if s == AT_BOUND:
                    pe.wait_ge(squares_ready, n + 1)
                    for i in range(2):
                        for h in range(2):
                            a_turn(turns)
                            pe.matmul(A[0:HEADS, :], head_mask_b[:, :], squares[:, i, h * HALF:(h + 1) * HALF],
                                      start=True, stop=True).then_inc(a_filled, 1)
                if s == AT_FLAG:
                    pe.wait_ge(before_done, (n + 1) * BEFORE_STEPS)
                    a_turn(turns)
                    pe.matmul(A[0:1, 0:1], above[:, :], ones_col[:, :], start=True, stop=True).then_inc(a_filled, 1)

            def row_maxima(n):
                for j in range(PAIRS):
                    pe.wait_ge(stack_in[j], 32 + 16 * STACK_DMAS * (n + 1))
                if not (isinstance(n, int) and n == 0):
                    pe.wait_ge(probs_ready, 2 * STEPS * n)
                for t in range(TILES):
                    for h in range(HEADS):
                        k = t * HEADS + h
                        if not (isinstance(n, int) and n == 0 and k < 2):
                            pe.wait_ge(max_drained, MAX_TILES * n + k - 1)
                        r = 64 * (h % 2)
                        for c in range(2):
                            mm = pe.matmul(S[:, k % 2, c * HALF:(c + 1) * HALF],
                                           Qs[r:r + MROW, h // 2, t * P:(t + 1) * P],
                                           Ks[r:r + MROW, h, c * HALF:(c + 1) * HALF], start=True, stop=True)
                        mm.then_inc(max_filled, 1)
                pe.wait_ge(max_drained, MAX_TILES * (n + 1))
                pe.sem_inc(pe_passed, 1)
                pe.transpose(S[0:MAX_TILES, 0, 0:P], mx[:, :], ident[:, :]).then_inc(max_turned, 1)
                pe.wait_ge(mneg_ready, n + 1)
                pe.wait_ge(mrow_in, 16 * HEADS * (n + 1))

            def scores(n, s, a):
                j, kb = s // TILES, s % TILES
                before = 2 * STEPS * n + 2 * s + a - 1
                if not (isinstance(before, int) and before <= 0):
                    pe.wait_ge(probs_ready, before)
                if kb == 0 and a == 0:
                    pe.wait_ge(stack_in[j], 32 + 16 * STACK_DMAS * (n + 1))
                for c in range(2):
                    mm = pe.matmul(S[:, a, c * HALF:(c + 1) * HALF], Ks[:, 2 * j + a, kb * P:(kb + 1) * P],
                                   Qs[:, j, c * HALF:(c + 1) * HALF], start=True, stop=True)
                mm.then_inc(scores_ready, 1)

            def weighted(n, s):
                j, kb = s // TILES, s % TILES
                pe.wait_ge(probs_ready, 2 * STEPS * n + 2 * s + 2)
                if kb == 0:
                    pe.wait_ge(va_ready, PAIRS * n + j + 1)
                    if not (isinstance(n, int) and n == 0 and j == 0):
                        pe.wait_ge(o_copied, PAIRS * n + j)
                for a in range(2):
                    for c in range(2):
                        r = 32 * (2 * a + c)
                        mm = pe.matmul(O[r:r + 32, :], Va[:, kb, 2 * j + a, :], Pr[:, s % 2, a, c * HALF:(c + 1) * HALF],
                                       start=(kb == 0), stop=(kb == TILES - 1))
                mm.then_inc(pv_done, 1)

            def turn_o(n, j, turns):
                pe.wait_ge(o_copied, PAIRS * n + j + 1)
                a_turn(turns)
                for t in range(4):
                    mm = pe.transpose(A[:, t * P:(t + 1) * P], Ot[:, t * P:(t + 1) * P], ident[:, :])
                mm.then_inc(a_filled, 1)

            def turn4(bank, filled, src, h):
                for t in range(4):
                    mm = pe.transpose(bank[:, t * P:(t + 1) * P], src[:, 4 * h + t, :], ident[:, :])
                mm.then_inc(filled, 1)

            def by_token(bank, filled, pairs, h):
                for t in range(4):
                    c = (4 * h + t) * P
                    for i, (lhs, w) in enumerate(pairs):
                        mm = pe.matmul(bank[:, t * P:(t + 1) * P], lhs[:, c:c + P], w, start=(i == 0),
                                       stop=(i == len(pairs) - 1))
                mm.then_inc(filled, 1)

            def after_tasks(n, s, attn_turn):
                if s == AT_AT:
                    pe.wait_ge(a_drained, attn_turn)
                    for h in range(2):
                        turn4(*b_turn(n, h), attn, h)
                if s == AT_TOK:
                    for h in range(2):
                        b_ready(n, h)
                        by_token(*b_turn(n, 2 + h), [(attnT, wow[:, :])], h)
                if s == AT_T:
                    pe.wait_ge(that_ready, 2 * n + 1)
                    for h in range(2):
                        turn4(*b_turn(n, 4 + h), that, h)
                if s == AT_Q1:
                    for h in range(2):
                        b_ready(n, 4 + h)
                        bank, filled = b_turn(n, 6 + h)
                        pe.matmul(bank[:, :], wq1_s[:, :], half(tT, h), start=True, stop=True).then_inc(filled, 1)
                if s == AT_PK:
                    pe.wait_ge(pooled_ready, n + 1)
                    bank, filled = b_turn(n, 8)
                    pe.matmul(bank[:, 0:POS], wkv1_s[:, 0:C], pooled[:, :], start=True, stop=True).then_inc(filled, 1)
                    bank, filled = b_turn(n, 9)
                    pe.matmul(bank[0:POS, 0:2 * C], pooled[:, :], wkv1_s[:, :], start=True, stop=True).then_inc(filled, 1)
                if AT_SC <= s < AT_SC + PAIRS:
                    j = s - AT_SC
                    if j == 0:
                        b_ready(n, 8)
                        b_ready(n, 6)
                        b_ready(n, 7)
                    for h in range(2):
                        bank, filled = b_turn(n, 10 + 2 * j + h)
                        pe.matmul(bank[:, :], bd_all[:, 2 * j:2 * j + 2, :].rearrange("p a b -> p (a b)"), half(q1T, h),
                                  start=True, stop=True).then_inc(filled, 1)
                if s == AT_RT:
                    b_ready(n, 17)
                    bank, filled = b_turn(n, 18)
                    pe.sem_inc(pe_passed, 1)
                    pe.transpose(bank[0:1, 0:P], r1[:, :], ident[:, :]).then_inc(filled, 1)
                if s == AT_RB:
                    b_ready(n, 18)
                    bank, filled = b_turn(n, 19)
                    pe.matmul(bank[0:POS, 0:POS], ones_row[:, :], red[:, :], start=True, stop=True).then_inc(filled, 1)
                if s == AT_SEL:
                    pe.wait_ge(hot_ready, n + 1)
                    bank, filled = b_turn(n, 20)
                    pe.matmul(bank[:, 0:TOPK], pkv[:, 0:C], hot[:, 0, :], start=True, stop=True).then_inc(filled, 1)
                    bank, filled = b_turn(n, 21)
                    pe.matmul(bank[:, 0:C], hot[:, :, :].rearrange("p a b -> p (a b)"), pkv[:, C:2 * C],
                              start=True, stop=True).then_inc(filled, 1)
                if s == AT_S2:
                    b_ready(n, 20)
                    for h in range(2):
                        by_token(*b_turn(n, 22 + h), [(q1T, bd_k[:, :, :].rearrange("p a b -> p (a b)"))], h)
                if s == AT_PT:
                    pe.wait_ge(e2_ready, n + 1)
                    for h in range(2):
                        turn4(*b_turn(n, 24 + h), E2[:, :, :].rearrange("p (t h) k -> p t (h k)", t=TILES), h)
                if s == AT_TOK2:
                    for h in range(2):
                        b_ready(n, 24 + h)
                        by_token(*b_turn(n, 26 + h), [(E2T, bd_v[:, :, :].rearrange("p a b -> p (a b)"))], h)
                if s == AT_TT2:
                    for h in range(2):
                        b_ready(n, 26 + h)
                        turn4(*b_turn(n, 28 + h), tok2, h)
                if s == AT_T2:
                    pe.wait_ge(that_ready, 2 * n + 2)
                    for h in range(2):
                        turn4(*b_turn(n, 30 + h), that, h)
                if s in (AT_FF, AT_FF + 1):
                    f = s - AT_FF
                    for h in range(2):
                        b_ready(n, 30 + h)
                        bank, filled = b_turn(n, 32 + 2 * f + h)
                        pe.matmul(bank[:, :], wf1_s[:, f * C:(f + 1) * C], half(tT, h), start=True, stop=True)\
                            .then_inc(filled, 1)
                if s == AT_OUT:
                    for h in range(2):
                        b_ready(n, 34 + h)
                        by_token(*b_turn(n, 36 + h), [(tok2T, wout_s[:, :]), (hT[:, 0, :], w2o[:, 0, :]),
                                                      (hT[:, 1, :], w2o[:, 1, :])], h)

            pe.wait_ge(weights_in, 16 * (WEIGHT_DMAS + 1))
            pe.wait_ge(consts, 2)
            pe.transpose(A[:, 0:P], wo_s[:, :], ident[:, :])
            pe.transpose(A[:, P:2 * P], wf2_s[:, 0, :], ident[:, :])
            pe.transpose(A[:, 2 * P:3 * P], wf2_s[:, 1, :], ident[:, :]).then_inc(setup_filled, 1)
            pe.wait_ge(vsetup, 5)
            pe.matmul(BC[0][:, 0:C], wT[:, 0, :], win_s[:, :], start=True, stop=True)
            pe.matmul(BC[0][:, C:2 * C], wT[:, 1, :], wout_s[:, :], start=True, stop=True)
            pe.matmul(BC[0][:, 2 * C:3 * C], wT[:, 2, :], wout_s[:, :], start=True, stop=True).then_inc(setup_filled, 1)
            pe.matmul(BC[1][:, 0:C], vecB[:, 0, :], win_s[:, :], start=True, stop=True)
            pe.matmul(BC[1][:, C:2 * C], vecB[:, 1, :], wout_s[:, :], start=True, stop=True).then_inc(setup_filled, 1)
            pe.wait_ge(vsetup, 9)

            turns = [0, 0]
            for s in range(STEPS):
                before_tasks(0, turns, s)

            def image(n, base, first=False, last=False):
                pe.wait_ge(a_drained, base)
                pe.sem_inc(pe_passed, 1)
                with pe.If(pe.value_load(flag[0:1, 0:1], min_val=0, max_val=HEADS) > 0):
                    row_maxima(n)
                with pe.Else():
                    pe.sem_inc(max_filled, MAX_TILES)
                    pe.sem_inc(max_turned, 1)
                turns = [base, 0]
                for s in range(STEPS):
                    scores(n, s, 0)
                    scores(n, s, 1)
                    if s > 0:
                        weighted(n, s - 1)
                    elif not first:
                        weighted(n - 1, STEPS - 1)
                    if s == 1 and not first:
                        turn_o(n - 1, PAIRS - 1, turns)
                    if s > 1 and s % TILES == 1:
                        turn_o(n, s // TILES - 1, turns)
                    if not last:
                        before_tasks(n + 1, turns, s)
                    if not first:
                        after_tasks(n - 1, s, base + 1)

            image(0, FIRST_TURNS, first=True)
            with pe.Fori(1, IMAGES - 1) as n:
                image(n, FIRST_TURNS + TURNS_0 + (n - 1) * TURNS)
            base = FIRST_TURNS + TURNS_0 + (IMAGES - 2) * TURNS
            image(IMAGES - 1, base, last=True)
            weighted(IMAGES - 1, STEPS - 1)
            turn_o(IMAGES - 1, PAIRS - 1, [base + PAIRS, 0])
            for s in range(STEPS):
                after_tasks(IMAGES - 1, s, base + PAIRS + 1)

        @block.scalar
        def _(act):
            def drain_a(turns):
                k = next_turn(turns)
                act.wait_ge(a_filled, k)

            def drain_b(n, k):
                act.wait_ge(b_filled[k % 2], n * (AFTER // 2) + k // 2 + 1)
                return BC[k % 2], b_drained[k % 2]

            def exps(n, s, a):
                act.wait_ge(scores_ready, 2 * STEPS * n + 2 * s + a + 1)
                used = STEPS * n + s - 1
                if a == 0 and not (isinstance(used, int) and used <= 0):
                    act.wait_ge(pv_done, used)
                act.activation(Pr[:, s % 2, a, :], S[:, a, :], ACT.Exp, scale=SCALE).then_inc(probs_ready, 1)

            def before_tasks(n, turns, s):
                if s == AT_XT:
                    for h in range(2):
                        drain_a(turns)
                        act.activation(half(xT, h), A[:, :], ACT.Copy).then_inc(a_drained, 1)
                if s == AT_XN:
                    for h in range(2):
                        drain_a(turns)
                        act.activation(half(xnT, h), A[:, :], ACT.Identity, bias=LNB, scale=LNS).then_inc(a_drained, 1)
                if s in (AT_TOKX, AT_Q, AT_K, AT_V):
                    next_turn(turns)
                    next_turn(turns)
                if s == AT_BOUND:
                    for _ in range(4):
                        next_turn(turns)
                if s == AT_FLAG:
                    next_turn(turns)

            def after_tasks(n, s):
                if s in (AT_T, AT_T2):
                    g, be, k0 = (G1, BE1, 4) if s == AT_T else (G2, BE2, 30)
                    for h in range(2):
                        bank, drained = drain_b(n, k0 + h)
                        act.activation(half(tT, h), bank[:, :], ACT.Identity, bias=be, scale=g).then_inc(drained, 1)
                if s in (AT_Q1, AT_PT, AT_TT2):
                    dst, k0 = {AT_Q1: (q1T, 6), AT_PT: (E2T, 24), AT_TT2: (tok2T, 28)}[s]
                    for h in range(2):
                        bank, drained = drain_b(n, k0 + h)
                        act.activation(half(dst, h), bank[:, :], ACT.Copy).then_inc(drained, 1)
                if s == AT_S2:
                    for h in range(2):
                        act.wait_ge(b_drained[h], n * (AFTER // 2) + 12)
                    act.activation(E2[:, :, :], E2[:, :, :], ACT.Exp, scale=SCALE).then_inc(e2_exp, 1)
                if s in (AT_FF, AT_FF + 1):
                    f = s - AT_FF
                    for h in range(2):
                        bank, drained = drain_b(n, 32 + 2 * f + h)
                        act.activation(hT[:, f, h * HALF:(h + 1) * HALF], bank[:, :], ACT.Gelu,
                                       bias=cols[:, 8 + f:9 + f]).then_inc(drained, 1)

            act.wait_ge(weights_in, 16 * (WEIGHT_DMAS + 1))
            turns = [0, 0]
            for s in range(STEPS):
                before_tasks(0, turns, s)

            def image(n, base, first=False, last=False):
                turns = [base, 0]
                for s in range(STEPS):
                    exps(n, s, 0)
                    exps(n, s, 1)
                    if (s == 1 and not first) or (s > 1 and s % TILES == 1):
                        next_turn(turns)
                    if not last:
                        before_tasks(n + 1, turns, s)
                    if not first:
                        after_tasks(n - 1, s)

            image(0, FIRST_TURNS, first=True)
            with act.Fori(1, IMAGES - 1) as n:
                image(n, FIRST_TURNS + TURNS_0 + (n - 1) * TURNS)
            image(IMAGES - 1, 0, last=True)
            for s in range(STEPS):
                after_tasks(IMAGES - 1, s)

        @block.vector
        def _(dve):
            def step(own, ins):
                ins.then_inc(own[0], 1)
                own[2] += 1
                dve.wait_ge(own[0], own[1] + own[2])

            def drain_a(turns):
                dve.wait_ge(a_filled, next_turn(turns))

            def drain_b(n, k):
                dve.wait_ge(b_filled[k % 2], n * (AFTER // 2) + k // 2 + 1)
                return BC[k % 2], b_drained[k % 2]

            def layer_norm(own, src, st, ln, eps, ready):
                for t in range(TILES):
                    ins = dve.bn_stats(st[:, t, :], src[:, t, :])
                step(own, ins)
                m_e, v_e, m_o, v_o = (st[:, :, i] for i in (1, 2, 4, 5))
                mean, y, d, v, w, g = (ln[:, i, :] for i in range(6))
                dve.tensor_tensor(mean, m_e, m_o, ALU.add)
                dve.tensor_tensor(v, v_e, v_o, ALU.add)
                step(own, dve.tensor_tensor(d, m_e, m_o, ALU.subtract))
                dve.tensor_scalar(mean, mean, 0.5, None, ALU.mult)
                dve.tensor_scalar(v, v, 1.0 / C, eps, ALU.mult, ALU.add)
                step(own, dve.scalar_tensor_tensor(out=w, in0=d, scalar=0.25, in1=d, op0=ALU.mult, op1=ALU.mult))
                step(own, dve.tensor_tensor(v, v, w, ALU.add))
                dve.tensor_scalar(w, v, -0.5, None, ALU.mult)
                step(own, dve.tensor_scalar(g.bitcast(i32), v.bitcast(i32), 1, None, ALU.logical_shift_right))
                step(own, dve.tensor_scalar(y.bitcast(i32), g.bitcast(i32), -1.0, RSQRT_MAGIC, ALU.mult, ALU.add))
                for k in range(3):
                    step(own, dve.tensor_tensor(g, y, y, ALU.mult))
                    step(own, dve.tensor_tensor(d, g, w, ALU.mult))
                    ins = dve.scalar_tensor_tensor(out=y, in0=d, scalar=1.5, in1=y, op0=ALU.add, op1=ALU.mult)
                    if k < 2:
                        step(own, ins)
                ins.then_inc(ready, 1)

            def before_tasks(n, turns, own, s):
                if s == AT_XT:
                    next_turn(turns)
                    next_turn(turns)
                if s == AT_TOKX:
                    if not (isinstance(n, int) and n == 0):
                        dve.wait_ge(tokx_moved, n)
                    for h in range(2):
                        drain_a(turns)
                        dve.tensor_tensor(tiles4(tokx_new, h), A[:, :].rearrange("p (t c) -> p t c", t=4),
                                          tok_bias[:, :].unsqueeze(1).to_broadcast([P, 4, C]), ALU.add).then_inc(a_drained, 1)
                    dve.wait_ge(x_in, 16 * (n + 1))
                    layer_norm(own, X, st0, ln0, LN0_EPS, ln0_ready)
                if s == AT_XN:
                    next_turn(turns)
                    next_turn(turns)
                if s in (AT_Q, AT_K):
                    hi, lo, bias = (qh, ql, BQ) if s == AT_Q else (kh, kl, BK)
                    if s == AT_Q and not (isinstance(n, int) and n == 0):
                        for j in range(PAIRS):
                            dve.wait_ge(stack_in[j], 32 + 16 * STACK_DMAS * n)
                    for h in range(2):
                        drain_a(turns)
                        step(own, dve.tensor_scalar(half(hi, h), A[:, :], bias, None, ALU.add))
                        dve.scalar_tensor_tensor(out=half(lo, h), in0=A[:, :], scalar=bias, in1=half(hi, h).bitcast(fp32),
                                                 op0=ALU.add, op1=ALU.subtract).then_inc(a_drained, 1)
                if s == AT_V:
                    if not (isinstance(n, int) and n == 0):
                        dve.wait_ge(va_ready, PAIRS * n)
                    for h in range(2):
                        drain_a(turns)
                        dve.tensor_tensor(tiles4(v_new, h), A[:, :].rearrange("p (t c) -> p t c", t=4),
                                          rows[:, 0:1, :].to_broadcast([P, 4, C]), ALU.add).then_inc(a_drained, 1)

                if s == AT_BOUND:
                    for i in range(4):
                        drain_a(turns)
                        dve.tensor_reduce(peak[:, i:i + 1], A[0:HEADS, :], AX.X, ALU.max).then_inc(a_drained, 1)
                    dve.wait_ge(a_drained, turns[0] + turns[1])
                    step(own, dve.tensor_reduce(peak[:, 4:6], peak[:, 0:4].rearrange("h (i c) -> h i c", i=2), AX.X, ALU.max))
                    step(own, dve.tensor_tensor(peak[:, 6:7], peak[:, 4:5], peak[:, 5:6], ALU.add))
                    step(own, dve.tensor_scalar(above[0:HEADS, :], peak[:, 6:7], SAFE_SQUARES, None, ALU.is_gt))
                if s == AT_FLAG:
                    drain_a(turns)
                    dve.tensor_copy(flag[:, :], A[0:1, 0:1]).then_inc(a_drained, 1)

            def row_maxima(n):
                for t in range(TILES):
                    for h in range(HEADS):
                        k = t * HEADS + h
                        dve.wait_ge(max_filled, MAX_TILES * n + k + 1)
                        dve.tensor_reduce(mx[:, h * TILES + t:h * TILES + t + 1], S[:, k % 2, :], AX.X, ALU.max)\
                            .then_inc(max_drained, 1)
                dve.wait_ge(max_turned, n + 1)
                dve.tensor_scalar(mneg[:, :], S[0:MAX_TILES, 0, 0:P], -1.0, None, ALU.mult).then_inc(mneg_ready, 1)

            def copy_o(n, j):
                dve.wait_ge(pv_done, STEPS * n + TILES * (j + 1))
                dve.tensor_copy(Ot[:, :], O[:, :]).then_inc(o_copied, 1)

            def divide_o(n, j, turns, own):
                drain_a(turns)
                o = A[:, :].rearrange("p (t a c e) -> p t a c e", t=4, a=2, c=2)
                r = rden[:, :].rearrange("p (t a c) -> p t a c", t=4, a=2)
                step(own, dve.reciprocal(rden[:, :].rearrange("p (u o) -> p u o", o=1),
                                        A[:, :].rearrange("p (u e) -> p u e", e=32)[:, :, HD:HD + 1]))
                for c in range(2):
                    ins = dve.tensor_tensor(
                        attn[:, 4 * c:4 * c + 4, 2 * HD * j:2 * HD * (j + 1)].rearrange("p t (a d) -> p t a d", a=2),
                        o[:, :, :, c, 0:HD], r[:, :, :, c:c + 1].to_broadcast([P, 4, 2, HD]), ALU.mult)
                ins.then_inc(a_drained, 1)

            def after_tasks(n, own, s):
                if s == AT_AT:
                    for h in range(2):
                        bank, drained = drain_b(n, h)
                        dve.tensor_copy(half(attnT, h), bank[:, :]).then_inc(drained, 1)
                if s == AT_TOK:
                    dve.wait_ge(tokx_moved, n + 1)
                    for h in range(2):
                        bank, drained = drain_b(n, 2 + h)
                        dve.tensor_tensor(flat4(tok, h), bank[:, :], flat4(tokx, h), ALU.add).then_inc(drained, 1)
                        dve.wait_ge(drained, n * (AFTER // 2) + 2)
                    layer_norm(own, tok, st1, ln1, LN1_EPS, ln1_ready)
                if s == AT_T:
                    for h in range(2):
                        dve.wait_ge(b_drained[h], n * (AFTER // 2) + 3)
                    step(own, dve.tensor_reduce(pooled[:, :].rearrange("p (y x) -> p y x", y=GRID),
                                               tT[:, :].rearrange("p (y a x b) -> p y x a b", y=GRID, a=POOL, x=GRID),
                                               AX.XY, ALU.add))
                    dve.tensor_scalar(pooled[:, :], pooled[:, :], 1.0 / POOL ** 2, None, ALU.mult).then_inc(pooled_ready, 1)
                if s == AT_PK:
                    bank, drained = drain_b(n, 8)
                    step(own, dve.tensor_copy(pkT[:, :], bank[:, 0:POS]))
                    dve.tensor_tensor(bd_all[:, :, :], pkT[:, :].unsqueeze(1).to_broadcast([P, HEADS, POS]),
                                      head_mask[:, :].unsqueeze(2).to_broadcast([P, HEADS, POS]), ALU.mult).then_inc(drained, 1)
                    bank, drained = drain_b(n, 9)
                    dve.tensor_copy(pkv[:, :], bank[0:POS, 0:2 * C]).then_inc(drained, 1)
                if AT_SC <= s < AT_SC + PAIRS:
                    j = s - AT_SC
                    for h in range(2):
                        k = 10 + 2 * j + h
                        bank, drained = drain_b(n, k)
                        ins = dve.tensor_reduce(r8[:, 2 * j + h:2 * j + h + 1], bank[:, :], AX.X, ALU.max)
                        if k < 17:
                            ins.then_inc(drained, 1)
                    if j == PAIRS - 1:
                        step(own, ins)
                        dve.tensor_reduce(r1[:, :], r8[:, :], AX.X, ALU.max).then_inc(b_drained[1], 1)
                if s == AT_RT:
                    bank, drained = drain_b(n, 18)
                    step(own, dve.tensor_copy(rrow[:, :], bank[0:1, 0:P]))
                    dve.tensor_tensor(red[:, :], rrow[:, 0:POS], rrow[:, POS:2 * POS], ALU.max).then_inc(drained, 1)
                if s == AT_RB:
                    bank, drained = drain_b(n, 19)
                    dve.tensor_copy(rB[:, :], bank[0:POS, 0:POS]).then_inc(drained, 1)
                    dve.wait_ge(drained, n * (AFTER // 2) + 10)
                    step(own, dve.tensor_tensor(rsel[:, :], rB[:, :], ident[0:POS, 0:POS], ALU.mult))
                    step(own, dve.tensor_reduce(rcol[:, :], rsel[:, :], AX.X, ALU.add))
                    dve.tensor_scalar(rgt[:, :], rB[:, :], rcol[:, 0:1], None, ALU.is_gt)
                    step(own, dve.scalar_tensor_tensor(out=rsel[:, :], in0=rB[:, :], scalar=rcol[:, 0:1], in1=below[:, :],
                                                      op0=ALU.is_equal, op1=ALU.mult))
                    step(own, dve.tensor_tensor(rgt[:, :], rgt[:, :], rsel[:, :], ALU.add))
                    step(own, dve.tensor_reduce(rank[:, :], rgt[:, :], AX.X, ALU.add))
                    dve.tensor_scalar(hot[:, :, :], iota_f[:, :].unsqueeze(1).to_broadcast([POS, HEADS, TOPK]),
                                      rank[:, 0:1], None, ALU.is_equal).then_inc(hot_ready, 1)
                if s == AT_SEL:
                    mask = head_mask[:, :].unsqueeze(2)
                    bank, drained = drain_b(n, 20)
                    dve.tensor_tensor(bd_k[:, :, :], bank[:, 0:TOPK].unsqueeze(1).to_broadcast([P, HEADS, TOPK]),
                                      mask.to_broadcast([P, HEADS, TOPK]), ALU.mult).then_inc(drained, 1)
                    bank, drained = drain_b(n, 21)
                    dve.tensor_tensor(bd_v[:, :, :], bank[:, 0:C].rearrange("p (h d) -> p h d", h=HEADS),
                                      mask.to_broadcast([P, HEADS, HD]), ALU.mult).then_inc(drained, 1)
                if s == AT_S2:
                    G = TILES * HEADS // 2
                    for h in range(2):
                        bank, drained = drain_b(n, 22 + h)
                        sc = bank[:, :].rearrange("p (g k) -> p g k", k=TOPK)
                        step(own, dve.tensor_reduce(m2[:, G * h:G * h + G], sc, AX.X, ALU.max))
                        ins = dve.tensor_tensor(E2[:, G * h:G * h + G, :], sc,
                                                m2[:, G * h:G * h + G].unsqueeze(2).to_broadcast([P, G, TOPK]), ALU.subtract)
                        ins.then_inc(drained, 1)
                    dve.wait_ge(e2_exp, n + 1)
                    step(own, dve.tensor_reduce(den2[:, :], E2[:, :, :], AX.X, ALU.add))
                    step(own, dve.reciprocal(m2[:, :], den2[:, :]))
                    dve.tensor_tensor(E2[:, :, :], E2[:, :, :], m2[:, :].unsqueeze(2).to_broadcast([P, 2 * G, TOPK]),
                                      ALU.mult).then_inc(e2_ready, 1)
                if s == AT_TOK2:
                    for h in range(2):
                        bank, drained = drain_b(n, 26 + h)
                        dve.tensor_tensor(flat4(tok2, h), bank[:, :], flat4(tok, h), ALU.add).then_inc(drained, 1)
                        dve.wait_ge(drained, n * (AFTER // 2) + 14)
                    layer_norm(own, tok2, st1, ln1, LN1_EPS, ln1_ready)
                if s == AT_OUT:
                    if not (isinstance(n, int) and n == 0):
                        dve.wait_ge(out_done, 16 * n)
                    for h in range(2):
                        bank, drained = drain_b(n, 36 + h)
                        dve.tensor_tensor(tiles4(Y, h), bank[:, :].rearrange("p (t c) -> p t c", t=4),
                                          out_bias[:, :].unsqueeze(1).to_broadcast([P, 4, C]), ALU.add).then_inc(drained, 1)

            dve.memset(ones_row[:, :], 1.0)
            dve.memset(ones_col[:, :], 1.0)
            dve.memset(above[:, :], 0.0)
            dve.memset(no_maximum[:, :], 0.0)
            dve.memset(k_ones[:, :], 1.0).then_inc(vsetup, 1)
            dve.wait_ge(consts, 8)
            dve.tensor_copy(head_mask_b[:, :], head_mask[:, :])
            dve.tensor_copy(iota_f[:, :], iota_i[:, :]).then_inc(vsetup, 1)
            dve.wait_ge(weights_in, 16 * (WEIGHT_DMAS + 1))
            dve.tensor_copy(vecB[:, 0, :], BO.to_broadcast([P, C])).then_inc(vsetup, 1)
            dve.tensor_copy(vecB[:, 1, :], BF2.to_broadcast([P, C])).then_inc(vsetup, 1)
            dve.wait_ge(setup_filled, 1)
            dve.tensor_copy(wT[:, :, :].rearrange("p a c -> p (a c)"), A[:, 0:3 * P]).then_inc(vsetup, 1)
            dve.wait_ge(setup_filled, 2)
            dve.tensor_copy(wow[:, :], BC[0][:, 0:C]).then_inc(vsetup, 1)
            dve.tensor_copy(w2o[:, :, :].rearrange("p a c -> p (a c)"), BC[0][:, C:3 * C]).then_inc(vsetup, 1)
            dve.wait_ge(setup_filled, 3)
            dve.tensor_tensor(tok_bias[:, :], BC[1][:, 0:C], rows[:, 1, :], ALU.add).then_inc(vsetup, 1)
            dve.tensor_tensor(out_bias[:, :], BC[1][:, C:2 * C], rows[:, 2, :], ALU.add).then_inc(vsetup, 1)
            dve.wait_ge(vsetup, 9)

            turns = [0, 0]
            own = [before_done, 0, 0]
            for s in range(STEPS):
                before_tasks(0, turns, own, s)

            def image(n, base, first=False, last=False):
                dve.wait_ge(a_drained, base)
                dve.sem_inc(dve_passed, 1)
                with dve.If(dve.value_load(flag[0:1, 0:1], min_val=0, max_val=HEADS) > 0):
                    row_maxima(n)
                with dve.Else():
                    dve.sem_inc(max_drained, MAX_TILES)
                    dve.sem_inc(mneg_ready, 1)
                turns = [base, 0]
                own_b = [before_done, (n + 1) * BEFORE_STEPS, 0]
                own_a = [after_done, (n - 1) * AFTER_STEPS if not first else 0, 0]
                own_o = [att_done, n * PAIRS - (0 if first else 1), 0]
                for s in range(STEPS):
                    if s == 0 and not first:
                        copy_o(n - 1, PAIRS - 1)
                    if s > 0 and s % TILES == 0:
                        copy_o(n, s // TILES - 1)
                    if s == 1 and not first:
                        divide_o(n - 1, PAIRS - 1, turns, own_o)
                    if s > 1 and s % TILES == 1:
                        divide_o(n, s // TILES - 1, turns, own_o)
                    if not last:
                        before_tasks(n + 1, turns, own_b, s)
                    if not first:
                        after_tasks(n - 1, own_a, s)
                assert last or own_b[2] == BEFORE_STEPS
                assert first or own_a[2] == AFTER_STEPS

            image(0, FIRST_TURNS, first=True)
            with dve.Fori(1, IMAGES - 1) as n:
                image(n, FIRST_TURNS + TURNS_0 + (n - 1) * TURNS)
            base = FIRST_TURNS + TURNS_0 + (IMAGES - 2) * TURNS
            image(IMAGES - 1, base, last=True)
            copy_o(IMAGES - 1, PAIRS - 1)
            divide_o(IMAGES - 1, PAIRS - 1, [base + PAIRS, 0], [att_done, IMAGES * PAIRS - 1, 0])
            own = [after_done, (IMAGES - 1) * AFTER_STEPS, 0]
            for s in range(STEPS):
                after_tasks(IMAGES - 1, own, s)


_INS = ['x', 'L0_conv_ln_scale', 'L0_conv_ln_bias', 'L0_conv_w_qkv', 'L0_conv_b_qkv', 'L0_conv_w_out', 'L0_conv_b_out',
        'L1_conv_Win', 'L1_conv_b_in', 'L1_conv_Wq', 'L1_conv_Wk', 'L1_conv_Wv', 'L1_conv_g1', 'L1_conv_be1',
        'L1_conv_g2', 'L1_conv_be2', 'L1_conv_Wf1', 'L1_conv_bf1', 'L1_conv_Wf2', 'L1_conv_bf2', 'L1_conv_Wout',
        'L1_conv_bout']
_OUTS = [((8, 32, 32, 128), 'float32')]


def kernel(**inputs):
    import numpy as _np
    import concourse.bacc as _bacc
    from concourse import mybir as _mybir
    from concourse.bass_utils import run_bass_kernel_spmd as _run

    nc = _bacc.Bacc("TRN2", target_bir_lowering=False, num_devices=1)
    arrays, args = {}, []
    for name in _INS:
        a = _np.ascontiguousarray(inputs[name])
        arrays[f"in_{name}_dram"] = a
        args.append(nc.dram_tensor(f"in_{name}_dram", a.shape, _mybir.dt.from_np(a.dtype), kind="ExternalInput").ap())
    for i, (shape, dtype) in enumerate(_OUTS):
        dt = _mybir.dt.from_np(_np.dtype(dtype))
        args.append(nc.dram_tensor(f"out_{i}_dram", shape, dt, kind="ExternalOutput").ap())
    two_layers(nc, *args)
    r = _run(nc, [arrays], core_ids=[0])
    got = tuple(r.results[0][f"out_{i}_dram"] for i in range(len(_OUTS)))
    return got[0]
```

```python
import concourse.bass as bass
from concourse import mybir
from contextlib import ExitStack

P = 128
IMAGES, SIDE, C = 8, 32, 128
T = SIDE * SIDE
TILES = T // P
HALF = 512
HEADS, HD = 8, 16
PAIRS = HEADS // 2
PARTS = 3
MROW = PARTS * HD
STEPS = PAIRS * TILES
POOL = 4
GRID = SIDE // POOL
POS = GRID * GRID
TOPK = 16
FF = 2 * C
SCALE = HD ** -0.5
SAFE_SQUARES = 60 / SCALE * 2 / 1.02
LN0_EPS, LN1_EPS = 1e-6, 1e-3
RSQRT_MAGIC = float(0x5F3759DF)

AT_LN0, AT_XT, AT_TOKX, AT_XN, AT_Q, AT_K, AT_V = 4, (2, 3), (6, 7), (10, 11), (12, 13), (14, 15), (16, 18)
AT_BOUND, AT_FLAG = (20, 21, 22, 23), 26
AT_AT, AT_TOK, AT_T, AT_Q1, AT_PK, AT_SC, AT_RT, AT_RB = 2, 3, 6, 7, 9, 10, 15, 16
AT_SEL, AT_S2, AT_PT, AT_TOK2, AT_TT2, AT_T2, AT_FF, AT_GELU, AT_OUT = 18, 19, 22, 23, 24, 26, (27, 28), 29, (30, 31)
AT_E2 = 20
AT_VA = (15, 18, 26)

BEFORE = 17
AFTER = 38
FIRST_TURNS = BEFORE
TURNS_0 = PAIRS - 1 + BEFORE
TURNS = PAIRS + BEFORE
KQ_TURN = 11
V_TURN = 14
BEFORE_STEPS = 21
AFTER_STEPS = 43


def two_layers(nc, x, ln_scale, ln_bias, w_qkv, b_qkv, w_out, b_out, Win, b_in, Wq, Wk, Wv, g1, be1, g2, be2,
               Wf1, bf1, Wf2, bf2, Wout, bout, out):
    fp32, f32r, bf16, i32 = mybir.dt.float32, mybir.dt.float32r, mybir.dt.bfloat16, mybir.dt.int32
    ALU = mybir.AluOpType
    ACT = mybir.ActivationFunctionType
    AX = mybir.AxisListType

    nc.disable_value_cache = True
    x_v = x.rearrange("n (t a) w c -> n (a w) t c", t=TILES)
    out_v = out.rearrange("n (t a) w c -> n (a w) t c", t=TILES)

    with ExitStack() as ctx:
        def sb(name, shape, dt=fp32):
            return ctx.enter_context(nc.sbuf_tensor(name, shape, dt))

        def sem(name):
            return ctx.enter_context(nc.semaphore(name))

        wqkv_s, wo_s, win_s = sb("wqkv_s", [P, 3 * C]), sb("wo_s", [P, C]), sb("win_s", [P, C])
        wq1_s, wkv1_s, wf1_s = sb("wq1_s", [P, C]), sb("wkv1_s", [P, 2 * C]), sb("wf1_s", [P, FF])
        wf2_s, wout_s = sb("wf2_s", [P, 2, C]), sb("wout_s", [P, C])
        cols = sb("cols", [P, 12])
        LNS, LNB, BQ, BK, G1, BE1, G2, BE2, BF1, BO, BF2 = (cols[:, i:i + 1] for i in (0, 1, 2, 3, 4, 5, 6, 7, 8, 10, 11))
        rows = sb("rows", [P, 3, C])
        wT = sb("wT", [P, 3, C])
        vecB = sb("vecB", [P, 2, C])
        wow = sb("wow", [P, C])
        w2o = sb("w2o", [P, 2, C])
        tok_bias, out_bias = sb("tok_bias", [P, C]), sb("out_bias", [P, C])
        ident = sb("ident", [P, P])
        head_mask = sb("head_mask", [P, HEADS])
        below = sb("below", [POS, POS])
        iota_i, iota_f = sb("iota_i", [POS, TOPK], i32), sb("iota_f", [POS, TOPK])
        ones_row, ones_col = sb("ones_row", [1, POS]), sb("ones_col", [P, 1])
        k_ones = sb("k_ones", [1, T])
        X, xn, xT, xnT = sb("X", [P, TILES, C]), sb("xn", [P, TILES, C]), sb("xT", [P, T]), sb("xnT", [P, T])
        squares, head_mask_b = sb("squares", [P, 2, T], bf16), sb("head_mask_b", [P, HEADS], bf16)
        peak, above, flag = sb("peak", [HEADS, 8]), sb("above", [P, 1]), sb("flag", [1, 1], i32)
        no_maximum = sb("no_maximum", [1, T])
        st0, ln0 = sb("st0", [P, TILES, 6]), sb("ln0", [P, 8, TILES])
        tokx_new, tokx = sb("tokx_new", [P, TILES, C]), sb("tokx", [P, TILES, C])
        qh, ql, kh, kl = (sb(n, [P, T], f32r) for n in ("qh", "ql", "kh", "kl"))
        v_new = sb("v_new", [P, TILES, C])
        Qs = sb("Qs", [P, PAIRS, T], f32r)
        Ks = sb("Ks", [P, HEADS, T], f32r)
        Va = sb("Va", [P, TILES, HEADS, 32])
        Pr = sb("Pr", [P, 2, 2, T])
        mx, mneg = sb("mx", [P, HEADS * TILES]), sb("mneg", [HEADS * TILES, P], f32r)
        Ot, rden = sb("Ot", [P, HALF]), sb("rden", [P, 16])
        attn, attnT = sb("attn", [P, TILES, C]), sb("attnT", [P, T])
        tok, that, tT, q1T = sb("tok", [P, TILES, C]), sb("that", [P, TILES, C]), sb("tT", [P, T]), sb("q1T", [P, T])
        st1, ln1 = sb("st1", [P, TILES, 6]), sb("ln1", [P, 8, TILES])
        pooled, pkT, pkv = sb("pooled", [P, POS]), sb("pkT", [P, POS]), sb("pkv", [POS, 2 * C])
        bd_all = sb("bd_all", [P, HEADS, POS])
        r8, r1, rrow, red = sb("r8", [P, 8]), sb("r1", [P, 1]), sb("rrow", [1, P]), sb("red", [1, POS])
        rB, rsel, rcol = sb("rB", [POS, POS]), sb("rsel", [POS, POS]), sb("rcol", [POS, 1])
        rgt, rank, hot = sb("rgt", [POS, POS]), sb("rank", [POS, 1]), sb("hot", [POS, HEADS, TOPK])
        bd_k, bd_v = sb("bd_k", [P, HEADS, TOPK]), sb("bd_v", [P, HEADS, HD])
        m2, den2 = sb("m2", [P, TILES * HEADS]), sb("den2", [P, TILES * HEADS])
        E2, E2T = sb("E2", [P, TILES * HEADS, TOPK]), sb("E2T", [P, T])
        tok2, tok2T = sb("tok2", [P, TILES, C]), sb("tok2T", [P, T])
        hT, Y = sb("hT", [P, 2, T]), sb("Y", [P, TILES, C])

        S = ctx.enter_context(nc.psum_tensor("S", [P, 2, T], fp32))
        O = ctx.enter_context(nc.psum_tensor("O", [P, HALF], fp32))
        A = ctx.enter_context(nc.psum_tensor("A", [P, HALF], fp32))
        BC = [ctx.enter_context(nc.psum_tensor(f"BC{i}", [P, HALF], fp32)) for i in range(2)]

        weights_in = sem("weights_in")
        consts = sem("consts")
        vsetup = sem("vsetup")
        setup_filled = sem("setup_filled")
        x_in = sem("x_in")
        a_filled, a_drained = sem("a_filled"), sem("a_drained")
        b_filled = [sem("b_filled"), sem("c_filled")]
        b_drained = [sem("b_drained"), sem("c_drained")]
        ln0_ready, xn_ready, that_ready = sem("ln0_ready"), sem("xn_ready"), sem("that_ready")
        before_done = sem("before_done")
        att_done = sem("att_done")
        after_done = sem("after_done")
        squares_ready = sem("squares_ready")
        tokx_moved = sem("tokx_moved")
        va_ready = sem("va_ready")
        stack_in = [sem(f"stack_in{j}") for j in range(PAIRS)]
        mrow_in = sem("mrow_in")
        max_filled, max_drained, mneg_ready, max_turned = sem("max_filled"), sem("max_drained"), sem("mneg_ready"), sem("max_turned")
        scores_ready, probs_ready, pv_done, o_copied = sem("scores_ready"), sem("probs_ready"), sem("pv_done"), sem("o_copied")
        e2_exp, e2_ready, gelu_ready = sem("e2_exp"), sem("e2_ready"), sem("gelu_ready")
        pooled_ready, hot_ready = sem("pooled_ready"), sem("hot_ready")
        out_done = sem("out_done")
        sp_passed, pool_passed, pe_passed, dve_passed = sem("sp_passed"), sem("pool_passed"), sem("pe_passed"), sem("dve_passed")

        STACK_DMAS = 2 * (2 * PARTS + 1)
        MAX_TILES = HEADS * TILES
        WEIGHT_DMAS = 8 + 12 + 3

        def next_turn(turns):
            turns[1] += 1
            return turns[0] + turns[1]

        def half(t, h):
            return t[:, h * HALF:(h + 1) * HALF]

        def tiles4(t, h):
            return t[:, 4 * h:4 * h + 4, :]

        def flat4(t, h):
            return tiles4(t, h).rearrange("p a c -> p (a c)")

        block = ctx.enter_context(nc.Block())

        @block.sync
        def _(sp):
            def load_x(n, xt_turns):
                if not (isinstance(n, int) and n == 0):
                    sp.wait_ge(xn_ready, n)
                    sp.wait_ge(a_drained, xt_turns)
                src = x_v[n] if isinstance(n, int) else x_v[bass.ds(n, 1)].rearrange("o p t c -> (o p) t c")
                sp.dma_start(X[:, :, :], src).then_inc(x_in, 16)

            def stack(n, j, turns_before):
                sp.wait_ge(a_drained, turns_before)
                if not (isinstance(n, int) and n == 0):
                    sp.wait_ge(scores_ready, 2 * STEPS * (n - 1) + 2 * TILES * (j + 1))
                for a in range(2):
                    r = HD * (2 * j + a)
                    for part, (q, k) in enumerate(((qh, kh), (qh, kl), (ql, kh))):
                        d = 64 * a + HD * part
                        sp.dma_start(Qs[d:d + HD, j, :].bitcast(fp32), q[r:r + HD, :].bitcast(fp32)).then_inc(stack_in[j], 16)
                        sp.dma_start(Ks[d:d + HD, 2 * j + a, :].bitcast(fp32), k[r:r + HD, :].bitcast(fp32)).then_inc(stack_in[j], 16)
                    d = 64 * a + MROW
                    sp.dma_start(Qs[d:d + 1, j, :].bitcast(fp32), no_maximum[:, :]).then_inc(stack_in[j], 16)

            def row_maximum(n):
                sp.wait_ge(mneg_ready, n + 1)
                for h in range(HEADS):
                    r = 64 * (h % 2) + MROW
                    sp.dma_start(Qs[r:r + 1, h // 2, :].rearrange("o (t q) -> o t q", t=TILES).bitcast(fp32),
                                 mneg[h * TILES:(h + 1) * TILES, :].bitcast(fp32)).then_inc(mrow_in, 16)

            def store(n):
                sp.wait_ge(b_drained[1], (n + 1) * (AFTER // 2))
                dst = out_v[n] if isinstance(n, int) else out_v[bass.ds(n, 1)].rearrange("o p t c -> (o p) t c")
                sp.dma_start(dst, Y[:, :, :]).then_inc(out_done, 16)

            for dst, src in ((wqkv_s[:, :], w_qkv), (wo_s[:, :], w_out), (win_s[:, :], Win), (wq1_s[:, :], Wq),
                             (wkv1_s[:, 0:C], Wk), (wkv1_s[:, C:2 * C], Wv), (wf1_s[:, :], Wf1),
                             (wf2_s[:, :, :], Wf2.rearrange("(a p) c -> p a c", a=2))):
                sp.dma_start(dst, src).then_inc(weights_in, 16)
            sp.dma_start(wout_s[:, :], Wout).then_inc(weights_in, 16)
            load_x(0, 0)
            col = lambda v, s: v[s:s + C].rearrange("(p o) -> p o", o=1)
            for dst, (v, s) in zip((LNS, LNB, BQ, BK, G1, BE1, G2, BE2, cols[:, 8:9], cols[:, 9:10], BO),
                                   ((ln_scale, 0), (ln_bias, 0), (b_qkv, 0), (b_qkv, C), (g1, 0), (be1, 0), (g2, 0),
                                    (be2, 0), (bf1, 0), (bf1, C), (b_out, 0))):
                sp.dma_start(dst, col(v, s)).then_inc(weights_in, 16)
            sp.dma_start(BF2, col(bf2, 0)).then_inc(weights_in, 16)
            for i, (v, s) in enumerate(((b_qkv, 2 * C), (b_in, 0))):
                sp.dma_start(rows[:, i, :], v[s:s + C].partition_broadcast(P)).then_inc(weights_in, 16)
            sp.dma_start(rows[:, 2, :], bout.partition_broadcast(P)).then_inc(weights_in, 16)
            sp.wait_ge(consts, 9)
            sp.wait_ge(vsetup, 1)
            for h in range(HEADS):
                r = 64 * (h % 2) + MROW
                sp.dma_start(Ks[r:r + 1, h, :].bitcast(fp32), k_ones[:, :]).then_inc(stack_in[h // 2], 16)
            load_x(1, 2)
            for j in range(PAIRS):
                stack(0, j, 10)

            def image(n, base, first=False, last=False, load=True):
                sp.wait_ge(a_drained, base)
                sp.sem_inc(sp_passed, 1)
                with sp.If(sp.value_load(flag[0:1, 0:1], min_val=0, max_val=HEADS) > 0):
                    row_maximum(n)
                with sp.Else():
                    sp.sem_inc(mrow_in, 16 * HEADS)
                k_turn = base + (0 if first else 1) + KQ_TURN
                if load and not last:
                    load_x(n + 2, base + (0 if first else 1) + 2)
                if not last:
                    for j in range(PAIRS - 1):
                        stack(n + 1, j, k_turn)
                if not first:
                    store(n - 1)
                if not last:
                    stack(n + 1, PAIRS - 1, k_turn)

            image(0, FIRST_TURNS, first=True)
            with sp.Fori(1, IMAGES - 2) as n:
                image(n, FIRST_TURNS + TURNS_0 + (n - 1) * TURNS)
            image(IMAGES - 2, FIRST_TURNS + TURNS_0 + (IMAGES - 3) * TURNS, load=False)
            image(IMAGES - 1, FIRST_TURNS + TURNS_0 + (IMAGES - 2) * TURNS, last=True)
            store(IMAGES - 1)
            sp.wait_ge(out_done, 16 * IMAGES)

        @block.gpsimd
        def _(pool):
            def wait(signal, value):
                pool.wait_ge(signal, value)
                pool.sem_inc(pool_passed, 1)

            def step(n, ins):
                ins.then_inc(consts, 1)
                pool.wait_ge(consts, n)

            step(1, pool.memset(ident[:, :], 0.0))
            step(2, pool.affine_select(out=ident[:, :], in_=ident[:, :], compare_op=ALU.not_equal, fill=1.0, base=0,
                                       pattern=[[-1, P]], channel_multiplier=1))
            step(3, pool.memset(head_mask[:, :], 1.0))
            step(4, pool.affine_select(out=head_mask[:, :], in_=head_mask[:, :], compare_op=ALU.is_ge, fill=0.0, base=0,
                                       pattern=[[-HD, HEADS]], channel_multiplier=1))
            step(5, pool.affine_select(out=head_mask[:, :], in_=head_mask[:, :], compare_op=ALU.is_ge, fill=0.0,
                                       base=HD - 1, pattern=[[HD, HEADS]], channel_multiplier=-1))
            step(6, pool.memset(below[:, :], 1.0))
            step(7, pool.affine_select(out=below[:, :], in_=below[:, :], compare_op=ALU.is_gt, fill=0.0, base=0,
                                       pattern=[[-1, POS]], channel_multiplier=1))
            step(8, pool.iota(iota_i[:, :], pattern=[[1, TOPK]], base=0, channel_multiplier=0))
            pool.memset(Ks[:, :, :].bitcast(fp32), 0.0)
            step(9, pool.memset(Qs[:, :, :].bitcast(fp32), 0.0))
            step(10, pool.memset(Va[:, :, :, :], 1.0))

            def normalise(dst, src, ln, ready, need, done):
                wait(ready, need)
                for t in range(TILES):
                    ins = pool.tensor_scalar(dst[:, t, :], src[:, t, :], ln[:, 0, t:t + 1], ln[:, 1, t:t + 1],
                                             ALU.subtract, ALU.mult)
                ins.then_inc(done, 1)

            def place_v(n, j, v_turn):
                wait(a_drained, v_turn)
                if not (isinstance(n, int) and n == 0):
                    wait(pv_done, STEPS * (n - 1) + TILES * (j + 1))
                pool.tensor_copy(Va[:, :, 2 * j:2 * j + 2, 0:HD],
                                 v_new[:, :, 2 * HD * j:2 * HD * (j + 1)].rearrange("p t (h d) -> p t h d", h=2))\
                    .then_inc(va_ready, 1)

            def square(n, k_turn):
                wait(a_drained, k_turn)
                for i, part in enumerate((qh, kh)):
                    ins = pool.tensor_tensor(squares[:, i, :], part[:, :].bitcast(fp32), part[:, :].bitcast(fp32), ALU.mult)
                ins.then_inc(squares_ready, 1)

            normalise(xn, X, ln0, ln0_ready, 1, xn_ready)
            square(0, 10)
            for j in range(PAIRS):
                place_v(0, j, 12)

            def image(n, base, first=False, last=False):
                v_turn = base + (0 if first else 1) + V_TURN
                if not first:
                    if not (isinstance(n, int) and n == 0):
                        place_v(n, PAIRS - 1, base)
                    wait(b_drained[1], (n - 1) * (AFTER // 2) + 2)
                wait(a_drained, base)
                pool.tensor_copy(tokx[:, :, :], tokx_new[:, :, :]).then_inc(tokx_moved, 1)
                if not last:
                    normalise(xn, X, ln0, ln0_ready, n + 2, xn_ready)
                    square(n + 1, v_turn - V_TURN + KQ_TURN)
                    place_v(n + 1, 0, v_turn)
                    place_v(n + 1, 1, v_turn)
                    place_v(n + 1, 2, v_turn)

            image(0, FIRST_TURNS, first=True)
            with pool.Fori(1, IMAGES - 1) as n:
                image(n, FIRST_TURNS + TURNS_0 + (n - 1) * TURNS)
            image(IMAGES - 1, FIRST_TURNS + TURNS_0 + (IMAGES - 2) * TURNS, last=True)

        @block.tensor
        def _(pe):
            def b_turn(n, k):
                b, before = k % 2, n * (AFTER // 2) + k // 2
                if not (isinstance(before, int) and before == 0):
                    pe.wait_ge(b_drained[b], before)
                return BC[b], b_filled[b]

            def b_ready(n, k):
                pe.wait_ge(b_drained[k % 2], n * (AFTER // 2) + k // 2 + 1)

            def a_turn(turns):
                k = next_turn(turns)
                if not (isinstance(k, int) and k == 1):
                    pe.wait_ge(a_drained, k - 1)

            def before_tasks(n, turns, s):
                if s in AT_XT:
                    h = AT_XT.index(s)
                    pe.wait_ge(x_in, 16 * (n + 1))
                    a_turn(turns)
                    for t in range(4):
                        mm = pe.transpose(A[:, t * P:(t + 1) * P], X[:, 4 * h + t, :], ident[:, :])
                    mm.then_inc(a_filled, 1)
                if s in AT_TOKX:
                    a_turn(turns)
                    by_token(A, a_filled, [(xT, win_s[:, :])], AT_TOKX.index(s))
                if s in AT_XN:
                    h = AT_XN.index(s)
                    pe.wait_ge(xn_ready, n + 1)
                    a_turn(turns)
                    for t in range(4):
                        mm = pe.transpose(A[:, t * P:(t + 1) * P], xn[:, 4 * h + t, :], ident[:, :])
                    mm.then_inc(a_filled, 1)
                if s in AT_Q + AT_K:
                    c, h = (0, AT_Q.index(s)) if s in AT_Q else (C, AT_K.index(s))
                    a_turn(turns)
                    pe.matmul(A[:, :], wqkv_s[:, c:c + C], half(xnT, h), start=True, stop=True).then_inc(a_filled, 1)
                if s in AT_V:
                    a_turn(turns)
                    by_token(A, a_filled, [(xnT, wqkv_s[:, 2 * C:3 * C])], AT_V.index(s))
                if s in AT_BOUND:
                    i, h = divmod(AT_BOUND.index(s), 2)
                    pe.wait_ge(squares_ready, n + 1)
                    a_turn(turns)
                    pe.matmul(A[0:HEADS, :], head_mask_b[:, :], squares[:, i, h * HALF:(h + 1) * HALF],
                              start=True, stop=True).then_inc(a_filled, 1)
                if s == AT_FLAG:
                    pe.wait_ge(before_done, (n + 1) * BEFORE_STEPS)
                    a_turn(turns)
                    pe.matmul(A[0:1, 0:1], above[:, :], ones_col[:, :], start=True, stop=True).then_inc(a_filled, 1)

            def row_maxima(n):
                for j in range(PAIRS):
                    pe.wait_ge(stack_in[j], 32 + 16 * STACK_DMAS * (n + 1))
                if not (isinstance(n, int) and n == 0):
                    pe.wait_ge(probs_ready, 2 * STEPS * n)
                for t in range(TILES):
                    for h in range(HEADS):
                        k = t * HEADS + h
                        if not (isinstance(n, int) and n == 0 and k < 2):
                            pe.wait_ge(max_drained, MAX_TILES * n + k - 1)
                        r = 64 * (h % 2)
                        for c in range(2):
                            mm = pe.matmul(S[:, k % 2, c * HALF:(c + 1) * HALF],
                                           Qs[r:r + MROW, h // 2, t * P:(t + 1) * P],
                                           Ks[r:r + MROW, h, c * HALF:(c + 1) * HALF], start=True, stop=True)
                        mm.then_inc(max_filled, 1)
                pe.wait_ge(max_drained, MAX_TILES * (n + 1))
                pe.sem_inc(pe_passed, 1)
                pe.transpose(S[0:MAX_TILES, 0, 0:P], mx[:, :], ident[:, :]).then_inc(max_turned, 1)
                pe.wait_ge(mneg_ready, n + 1)
                pe.wait_ge(mrow_in, 16 * HEADS * (n + 1))

            def scores(n, s, a):
                j, kb = s // TILES, s % TILES
                before = 2 * STEPS * n + 2 * s + a - 1
                if not (isinstance(before, int) and before <= 0):
                    pe.wait_ge(probs_ready, before)
                if kb == 0 and a == 0:
                    pe.wait_ge(stack_in[j], 32 + 16 * STACK_DMAS * (n + 1))
                for c in range(2):
                    mm = pe.matmul(S[:, a, c * HALF:(c + 1) * HALF], Ks[:, 2 * j + a, kb * P:(kb + 1) * P],
                                   Qs[:, j, c * HALF:(c + 1) * HALF], start=True, stop=True)
                mm.then_inc(scores_ready, 1)

            def weighted(n, s):
                j, kb = s // TILES, s % TILES
                pe.wait_ge(probs_ready, 2 * STEPS * n + 2 * s + 2)
                if kb == 0:
                    pe.wait_ge(va_ready, PAIRS * n + j + 1)
                    if not (isinstance(n, int) and n == 0 and j == 0):
                        pe.wait_ge(o_copied, PAIRS * n + j)
                for a in range(2):
                    for c in range(2):
                        r = 32 * (2 * a + c)
                        mm = pe.matmul(O[r:r + 32, :], Va[:, kb, 2 * j + a, :], Pr[:, s % 2, a, c * HALF:(c + 1) * HALF],
                                       start=(kb == 0), stop=(kb == TILES - 1))
                mm.then_inc(pv_done, 1)

            def turn_o(n, j, turns):
                pe.wait_ge(o_copied, PAIRS * n + j + 1)
                a_turn(turns)
                for t in range(4):
                    mm = pe.transpose(A[:, t * P:(t + 1) * P], Ot[:, t * P:(t + 1) * P], ident[:, :])
                mm.then_inc(a_filled, 1)

            def turn4(bank, filled, src, h):
                for t in range(4):
                    mm = pe.transpose(bank[:, t * P:(t + 1) * P], src[:, 4 * h + t, :], ident[:, :])
                mm.then_inc(filled, 1)

            def by_token(bank, filled, pairs, h):
                for t in range(4):
                    c = (4 * h + t) * P
                    for i, (lhs, w) in enumerate(pairs):
                        mm = pe.matmul(bank[:, t * P:(t + 1) * P], lhs[:, c:c + P], w, start=(i == 0),
                                       stop=(i == len(pairs) - 1))
                mm.then_inc(filled, 1)

            def after_tasks(n, s, attn_turn):
                if s == AT_AT:
                    pe.wait_ge(a_drained, attn_turn)
                    for h in range(2):
                        turn4(*b_turn(n, h), attn, h)
                if s == AT_TOK:
                    for h in range(2):
                        b_ready(n, h)
                        by_token(*b_turn(n, 2 + h), [(attnT, wow[:, :])], h)
                if s == AT_T:
                    pe.wait_ge(that_ready, 2 * n + 1)
                    for h in range(2):
                        turn4(*b_turn(n, 4 + h), that, h)
                if s == AT_Q1:
                    for h in range(2):
                        b_ready(n, 4 + h)
                        bank, filled = b_turn(n, 6 + h)
                        pe.matmul(bank[:, :], wq1_s[:, :], half(tT, h), start=True, stop=True).then_inc(filled, 1)
                if s == AT_PK:
                    pe.wait_ge(pooled_ready, n + 1)
                    bank, filled = b_turn(n, 8)
                    pe.matmul(bank[:, 0:POS], wkv1_s[:, 0:C], pooled[:, :], start=True, stop=True).then_inc(filled, 1)
                    bank, filled = b_turn(n, 9)
                    pe.matmul(bank[0:POS, 0:2 * C], pooled[:, :], wkv1_s[:, :], start=True, stop=True).then_inc(filled, 1)
                if AT_SC <= s < AT_SC + PAIRS:
                    j = s - AT_SC
                    if j == 0:
                        b_ready(n, 8)
                        b_ready(n, 6)
                        b_ready(n, 7)
                    for h in range(2):
                        bank, filled = b_turn(n, 10 + 2 * j + h)
                        pe.matmul(bank[:, :], bd_all[:, 2 * j:2 * j + 2, :].rearrange("p a b -> p (a b)"), half(q1T, h),
                                  start=True, stop=True).then_inc(filled, 1)
                if s == AT_RT:
                    b_ready(n, 17)
                    bank, filled = b_turn(n, 18)
                    pe.sem_inc(pe_passed, 1)
                    pe.transpose(bank[0:1, 0:P], r1[:, :], ident[:, :]).then_inc(filled, 1)
                if s == AT_RB:
                    b_ready(n, 18)
                    bank, filled = b_turn(n, 19)
                    pe.matmul(bank[0:POS, 0:POS], ones_row[:, :], red[:, :], start=True, stop=True).then_inc(filled, 1)
                if s == AT_SEL:
                    pe.wait_ge(hot_ready, n + 1)
                    bank, filled = b_turn(n, 20)
                    pe.matmul(bank[:, 0:TOPK], pkv[:, 0:C], hot[:, 0, :], start=True, stop=True).then_inc(filled, 1)
                    bank, filled = b_turn(n, 21)
                    pe.matmul(bank[:, 0:C], hot[:, :, :].rearrange("p a b -> p (a b)"), pkv[:, C:2 * C],
                              start=True, stop=True).then_inc(filled, 1)
                if s == AT_S2:
                    b_ready(n, 20)
                    for h in range(2):
                        by_token(*b_turn(n, 22 + h), [(q1T, bd_k[:, :, :].rearrange("p a b -> p (a b)"))], h)
                if s == AT_PT:
                    pe.wait_ge(e2_ready, n + 1)
                    for h in range(2):
                        turn4(*b_turn(n, 24 + h), E2[:, :, :].rearrange("p (t h) k -> p t (h k)", t=TILES), h)
                if s == AT_TOK2:
                    for h in range(2):
                        b_ready(n, 24 + h)
                        by_token(*b_turn(n, 26 + h), [(E2T, bd_v[:, :, :].rearrange("p a b -> p (a b)"))], h)
                if s == AT_TT2:
                    for h in range(2):
                        b_ready(n, 26 + h)
                        turn4(*b_turn(n, 28 + h), tok2, h)
                if s == AT_T2:
                    pe.wait_ge(that_ready, 2 * n + 2)
                    for h in range(2):
                        turn4(*b_turn(n, 30 + h), that, h)
                if s in AT_FF:
                    f = AT_FF.index(s)
                    for h in range(2):
                        b_ready(n, 30 + h)
                        bank, filled = b_turn(n, 32 + 2 * f + h)
                        pe.matmul(bank[:, :], wf1_s[:, f * C:(f + 1) * C], half(tT, h), start=True, stop=True)\
                            .then_inc(filled, 1)
                if s == AT_GELU:
                    for h in range(2):
                        bank, filled = b_turn(n, 36 + h)
                        for t in range(4):
                            c = (4 * h + t) * P
                            pe.matmul(bank[:, t * P:(t + 1) * P], tok2T[:, c:c + P], wout_s[:, :],
                                      start=(t == 0), stop=False)
                if s in AT_OUT:
                    h = AT_OUT.index(s)
                    if h == 0:
                        pe.wait_ge(gelu_ready, n + 1)
                    for t in range(4):
                        c = (4 * h + t) * P
                        for f in range(2):
                            mm = pe.matmul(BC[h][:, t * P:(t + 1) * P], hT[:, f, c:c + P], w2o[:, f, :],
                                           start=False, stop=(t == 3 and f == 1))
                    mm.then_inc(b_filled[h], 1)

            pe.wait_ge(weights_in, 16 * (WEIGHT_DMAS + 1))
            pe.wait_ge(consts, 2)
            pe.transpose(A[:, 0:P], wo_s[:, :], ident[:, :])
            pe.transpose(A[:, P:2 * P], wf2_s[:, 0, :], ident[:, :])
            pe.transpose(A[:, 2 * P:3 * P], wf2_s[:, 1, :], ident[:, :]).then_inc(setup_filled, 1)
            pe.wait_ge(vsetup, 5)
            pe.matmul(BC[0][:, 0:C], wT[:, 0, :], win_s[:, :], start=True, stop=True)
            pe.matmul(BC[0][:, C:2 * C], wT[:, 1, :], wout_s[:, :], start=True, stop=True)
            pe.matmul(BC[0][:, 2 * C:3 * C], wT[:, 2, :], wout_s[:, :], start=True, stop=True).then_inc(setup_filled, 1)
            pe.matmul(BC[1][:, 0:C], vecB[:, 0, :], win_s[:, :], start=True, stop=True)
            pe.matmul(BC[1][:, C:2 * C], vecB[:, 1, :], wout_s[:, :], start=True, stop=True).then_inc(setup_filled, 1)
            pe.wait_ge(vsetup, 9)

            turns = [0, 0]
            for s in range(STEPS):
                before_tasks(0, turns, s)

            def image(n, base, first=False, last=False):
                pe.wait_ge(a_drained, base)
                pe.sem_inc(pe_passed, 1)
                with pe.If(pe.value_load(flag[0:1, 0:1], min_val=0, max_val=HEADS) > 0):
                    row_maxima(n)
                with pe.Else():
                    pe.sem_inc(max_filled, MAX_TILES)
                    pe.sem_inc(max_turned, 1)
                turns = [base, 0]
                for s in range(STEPS):
                    scores(n, s, 0)
                    scores(n, s, 1)
                    if s == 1 and not first:
                        turn_o(n - 1, PAIRS - 1, turns)
                    if s > 1 and s % TILES == 1:
                        turn_o(n, s // TILES - 1, turns)
                    if not last:
                        before_tasks(n + 1, turns, s)
                    if not first:
                        after_tasks(n - 1, s, base + 1)
                    if s > 0:
                        weighted(n, s - 1)
                    elif not first:
                        weighted(n - 1, STEPS - 1)

            image(0, FIRST_TURNS, first=True)
            with pe.Fori(1, IMAGES - 1) as n:
                image(n, FIRST_TURNS + TURNS_0 + (n - 1) * TURNS)
            base = FIRST_TURNS + TURNS_0 + (IMAGES - 2) * TURNS
            image(IMAGES - 1, base, last=True)
            weighted(IMAGES - 1, STEPS - 1)
            turn_o(IMAGES - 1, PAIRS - 1, [base + PAIRS, 0])
            for s in range(STEPS):
                after_tasks(IMAGES - 1, s, base + PAIRS + 1)

        @block.scalar
        def _(act):
            def drain_a(turns):
                k = next_turn(turns)
                act.wait_ge(a_filled, k)

            def drain_b(n, k):
                act.wait_ge(b_filled[k % 2], n * (AFTER // 2) + k // 2 + 1)
                return BC[k % 2], b_drained[k % 2]

            def exps(n, s, a):
                act.wait_ge(scores_ready, 2 * STEPS * n + 2 * s + a + 1)
                used = STEPS * n + s - 1
                if a == 0 and not (isinstance(used, int) and used <= 0):
                    act.wait_ge(pv_done, used)
                act.activation(Pr[:, s % 2, a, :], S[:, a, :], ACT.Exp, scale=SCALE).then_inc(probs_ready, 1)

            def before_tasks(n, turns, s):
                if s in AT_XT:
                    drain_a(turns)
                    act.activation(half(xT, AT_XT.index(s)), A[:, :], ACT.Copy).then_inc(a_drained, 1)
                if s in AT_XN:
                    drain_a(turns)
                    act.activation(half(xnT, AT_XN.index(s)), A[:, :], ACT.Identity, bias=LNB, scale=LNS)\
                        .then_inc(a_drained, 1)
                if s in AT_TOKX + AT_Q + AT_K + AT_V + AT_BOUND + (AT_FLAG,):
                    next_turn(turns)

            def after_tasks(n, s):
                if s in (AT_T, AT_T2):
                    g, be, k0 = (G1, BE1, 4) if s == AT_T else (G2, BE2, 30)
                    for h in range(2):
                        bank, drained = drain_b(n, k0 + h)
                        act.activation(half(tT, h), bank[:, :], ACT.Identity, bias=be, scale=g).then_inc(drained, 1)
                if s in (AT_Q1, AT_PT, AT_TT2):
                    dst, k0 = {AT_Q1: (q1T, 6), AT_PT: (E2T, 24), AT_TT2: (tok2T, 28)}[s]
                    for h in range(2):
                        bank, drained = drain_b(n, k0 + h)
                        act.activation(half(dst, h), bank[:, :], ACT.Copy).then_inc(drained, 1)
                if s == AT_S2:
                    for h in range(2):
                        act.wait_ge(b_drained[h], n * (AFTER // 2) + 12)
                    act.activation(E2[:, :, :], E2[:, :, :], ACT.Exp, scale=SCALE).then_inc(e2_exp, 1)
                if s == AT_GELU:
                    for h in range(2):
                        act.wait_ge(b_drained[h], n * (AFTER // 2) + 18)
                    act.activation(hT[:, :, :], hT[:, :, :], ACT.Gelu).then_inc(gelu_ready, 1)

            act.wait_ge(weights_in, 16 * (WEIGHT_DMAS + 1))
            turns = [0, 0]
            for s in range(STEPS):
                before_tasks(0, turns, s)

            def image(n, base, first=False, last=False):
                turns = [base, 0]
                for s in range(STEPS):
                    exps(n, s, 0)
                    exps(n, s, 1)
                    if (s == 1 and not first) or (s > 1 and s % TILES == 1):
                        next_turn(turns)
                    if not last:
                        before_tasks(n + 1, turns, s)
                    if not first:
                        after_tasks(n - 1, s)

            image(0, FIRST_TURNS, first=True)
            with act.Fori(1, IMAGES - 1) as n:
                image(n, FIRST_TURNS + TURNS_0 + (n - 1) * TURNS)
            image(IMAGES - 1, 0, last=True)
            for s in range(STEPS):
                after_tasks(IMAGES - 1, s)

        @block.vector
        def _(dve):
            def step(own, ins):
                ins.then_inc(own[0], 1)
                own[2] += 1
                dve.wait_ge(own[0], own[1] + own[2])

            def drain_a(turns):
                dve.wait_ge(a_filled, next_turn(turns))

            def drain_b(n, k):
                dve.wait_ge(b_filled[k % 2], n * (AFTER // 2) + k // 2 + 1)
                return BC[k % 2], b_drained[k % 2]

            def layer_norm(own, src, st, ln, eps, ready):
                for t in range(TILES):
                    ins = dve.bn_stats(st[:, t, :], src[:, t, :])
                step(own, ins)
                m_e, v_e, m_o, v_o = (st[:, :, i] for i in (1, 2, 4, 5))
                mean, y, d, v, w, g = (ln[:, i, :] for i in range(6))
                dve.tensor_tensor(mean, m_e, m_o, ALU.add)
                dve.tensor_tensor(v, v_e, v_o, ALU.add)
                step(own, dve.tensor_tensor(d, m_e, m_o, ALU.subtract))
                dve.tensor_scalar(mean, mean, 0.5, None, ALU.mult)
                dve.tensor_scalar(v, v, 1.0 / C, eps, ALU.mult, ALU.add)
                step(own, dve.scalar_tensor_tensor(out=w, in0=d, scalar=0.25, in1=d, op0=ALU.mult, op1=ALU.mult))
                step(own, dve.tensor_tensor(v, v, w, ALU.add))
                dve.tensor_scalar(w, v, -0.5, None, ALU.mult)
                step(own, dve.tensor_scalar(g.bitcast(i32), v.bitcast(i32), 1, None, ALU.logical_shift_right))
                step(own, dve.tensor_scalar(y.bitcast(i32), g.bitcast(i32), -1.0, RSQRT_MAGIC, ALU.mult, ALU.add))
                for k in range(3):
                    step(own, dve.tensor_tensor(g, y, y, ALU.mult))
                    step(own, dve.tensor_tensor(d, g, w, ALU.mult))
                    ins = dve.scalar_tensor_tensor(out=y, in0=d, scalar=1.5, in1=y, op0=ALU.add, op1=ALU.mult)
                    if k < 2:
                        step(own, ins)
                ins.then_inc(ready, 1)

            def before_tasks(n, turns, own, s):
                if s in AT_XT + AT_XN:
                    next_turn(turns)
                if s == AT_LN0:
                    dve.wait_ge(x_in, 16 * (n + 1))
                    layer_norm(own, X, st0, ln0, LN0_EPS, ln0_ready)
                if s in AT_TOKX:
                    if not (isinstance(n, int) and n == 0):
                        dve.wait_ge(tokx_moved, n)
                    drain_a(turns)
                    dve.tensor_tensor(tiles4(tokx_new, AT_TOKX.index(s)), A[:, :].rearrange("p (t c) -> p t c", t=4),
                                      tok_bias[:, :].unsqueeze(1).to_broadcast([P, 4, C]), ALU.add).then_inc(a_drained, 1)
                if s in AT_Q + AT_K:
                    hi, lo, bias, h = (qh, ql, BQ, AT_Q.index(s)) if s in AT_Q else (kh, kl, BK, AT_K.index(s))
                    if s == AT_Q[0] and not (isinstance(n, int) and n == 0):
                        for j in range(PAIRS):
                            dve.wait_ge(stack_in[j], 32 + 16 * STACK_DMAS * n)
                    drain_a(turns)
                    step(own, dve.tensor_scalar(half(hi, h), A[:, :], bias, None, ALU.add))
                    dve.scalar_tensor_tensor(out=half(lo, h), in0=A[:, :], scalar=bias, in1=half(hi, h).bitcast(fp32),
                                             op0=ALU.add, op1=ALU.subtract).then_inc(a_drained, 1)
                if s in AT_V:
                    if not (isinstance(n, int) and n == 0):
                        dve.wait_ge(va_ready, PAIRS * n)
                    drain_a(turns)
                    dve.tensor_tensor(tiles4(v_new, AT_V.index(s)), A[:, :].rearrange("p (t c) -> p t c", t=4),
                                      rows[:, 0:1, :].to_broadcast([P, 4, C]), ALU.add).then_inc(a_drained, 1)
                if s in AT_BOUND:
                    i = AT_BOUND.index(s)
                    drain_a(turns)
                    dve.tensor_reduce(peak[:, i:i + 1], A[0:HEADS, :], AX.X, ALU.max).then_inc(a_drained, 1)
                if s == AT_BOUND[3]:
                    dve.wait_ge(a_drained, turns[0] + turns[1])
                    step(own, dve.tensor_reduce(peak[:, 4:6], peak[:, 0:4].rearrange("h (i c) -> h i c", i=2), AX.X, ALU.max))
                    step(own, dve.tensor_tensor(peak[:, 6:7], peak[:, 4:5], peak[:, 5:6], ALU.add))
                    step(own, dve.tensor_scalar(above[0:HEADS, :], peak[:, 6:7], SAFE_SQUARES, None, ALU.is_gt))
                if s == AT_FLAG:
                    if not (isinstance(n, int) and n == 0):
                        dve.wait_ge(mrow_in, 16 * HEADS * n)
                    drain_a(turns)
                    dve.tensor_copy(flag[:, :], A[0:1, 0:1]).then_inc(a_drained, 1)

            def row_maxima(n):
                for t in range(TILES):
                    for h in range(HEADS):
                        k = t * HEADS + h
                        dve.wait_ge(max_filled, MAX_TILES * n + k + 1)
                        dve.tensor_reduce(mx[:, h * TILES + t:h * TILES + t + 1], S[:, k % 2, :], AX.X, ALU.max)\
                            .then_inc(max_drained, 1)
                dve.wait_ge(max_turned, n + 1)
                dve.tensor_scalar(mneg[:, :], S[0:MAX_TILES, 0, 0:P], -1.0, None, ALU.mult).then_inc(mneg_ready, 1)

            def copy_o(n, j):
                dve.wait_ge(pv_done, STEPS * n + TILES * (j + 1))
                dve.tensor_copy(Ot[:, :], O[:, :]).then_inc(o_copied, 1)

            def divide_o(n, j, turns, own):
                drain_a(turns)
                o = A[:, :].rearrange("p (t a c e) -> p t a c e", t=4, a=2, c=2)
                r = rden[:, :].rearrange("p (t a c) -> p t a c", t=4, a=2)
                step(own, dve.reciprocal(rden[:, :].rearrange("p (u o) -> p u o", o=1),
                                        A[:, :].rearrange("p (u e) -> p u e", e=32)[:, :, HD:HD + 1]))
                for c in range(2):
                    ins = dve.tensor_tensor(
                        attn[:, 4 * c:4 * c + 4, 2 * HD * j:2 * HD * (j + 1)].rearrange("p t (a d) -> p t a d", a=2),
                        o[:, :, :, c, 0:HD], r[:, :, :, c:c + 1].to_broadcast([P, 4, 2, HD]), ALU.mult)
                ins.then_inc(a_drained, 1)

            def after_tasks(n, own, s):
                if s == AT_AT:
                    for h in range(2):
                        bank, drained = drain_b(n, h)
                        dve.tensor_copy(half(attnT, h), bank[:, :]).then_inc(drained, 1)
                if s == AT_TOK:
                    dve.wait_ge(tokx_moved, n + 1)
                    for h in range(2):
                        bank, drained = drain_b(n, 2 + h)
                        dve.tensor_tensor(flat4(tok, h), bank[:, :], flat4(tokx, h), ALU.add).then_inc(drained, 1)
                        dve.wait_ge(drained, n * (AFTER // 2) + 2)
                    layer_norm(own, tok, st1, ln1, LN1_EPS, after_done)
                    own[2] += 1
                    dve.wait_ge(own[0], own[1] + own[2])
                    for t in range(TILES):
                        ins = dve.tensor_scalar(that[:, t, :], tok[:, t, :], ln1[:, 0, t:t + 1], ln1[:, 1, t:t + 1],
                                                ALU.subtract, ALU.mult)
                    ins.then_inc(that_ready, 1)
                if s == AT_T:
                    for h in range(2):
                        dve.wait_ge(b_drained[h], n * (AFTER // 2) + 3)
                    step(own, dve.tensor_reduce(pooled[:, :].rearrange("p (y x) -> p y x", y=GRID),
                                               tT[:, :].rearrange("p (y a x b) -> p y x a b", y=GRID, a=POOL, x=GRID),
                                               AX.XY, ALU.add))
                    dve.tensor_scalar(pooled[:, :], pooled[:, :], 1.0 / POOL ** 2, None, ALU.mult).then_inc(pooled_ready, 1)
                if s == AT_PK:
                    bank, drained = drain_b(n, 8)
                    step(own, dve.tensor_copy(pkT[:, :], bank[:, 0:POS]))
                    dve.tensor_tensor(bd_all[:, :, :], pkT[:, :].unsqueeze(1).to_broadcast([P, HEADS, POS]),
                                      head_mask[:, :].unsqueeze(2).to_broadcast([P, HEADS, POS]), ALU.mult).then_inc(drained, 1)
                    bank, drained = drain_b(n, 9)
                    dve.tensor_copy(pkv[:, :], bank[0:POS, 0:2 * C]).then_inc(drained, 1)
                if AT_SC <= s < AT_SC + PAIRS:
                    j = s - AT_SC
                    for h in range(2):
                        k = 10 + 2 * j + h
                        bank, drained = drain_b(n, k)
                        ins = dve.tensor_reduce(r8[:, 2 * j + h:2 * j + h + 1], bank[:, :], AX.X, ALU.max)
                        if k < 17:
                            ins.then_inc(drained, 1)
                    if j == PAIRS - 1:
                        step(own, ins)
                        dve.tensor_reduce(r1[:, :], r8[:, :], AX.X, ALU.max).then_inc(b_drained[1], 1)
                if s == AT_RT:
                    bank, drained = drain_b(n, 18)
                    step(own, dve.tensor_copy(rrow[:, :], bank[0:1, 0:P]))
                    dve.tensor_tensor(red[:, :], rrow[:, 0:POS], rrow[:, POS:2 * POS], ALU.max).then_inc(drained, 1)
                if s == AT_RB:
                    bank, drained = drain_b(n, 19)
                    dve.tensor_copy(rB[:, :], bank[0:POS, 0:POS]).then_inc(drained, 1)
                    dve.wait_ge(drained, n * (AFTER // 2) + 10)
                    step(own, dve.tensor_tensor(rsel[:, :], rB[:, :], ident[0:POS, 0:POS], ALU.mult))
                    step(own, dve.tensor_reduce(rcol[:, :], rsel[:, :], AX.X, ALU.add))
                    dve.tensor_scalar(rgt[:, :], rB[:, :], rcol[:, 0:1], None, ALU.is_gt)
                    step(own, dve.scalar_tensor_tensor(out=rsel[:, :], in0=rB[:, :], scalar=rcol[:, 0:1], in1=below[:, :],
                                                      op0=ALU.is_equal, op1=ALU.mult))
                    step(own, dve.tensor_tensor(rgt[:, :], rgt[:, :], rsel[:, :], ALU.add))
                    step(own, dve.tensor_reduce(rank[:, :], rgt[:, :], AX.X, ALU.add))
                    dve.tensor_scalar(hot[:, :, :], iota_f[:, :].unsqueeze(1).to_broadcast([POS, HEADS, TOPK]),
                                      rank[:, 0:1], None, ALU.is_equal).then_inc(hot_ready, 1)
                if s == AT_SEL:
                    mask = head_mask[:, :].unsqueeze(2)
                    bank, drained = drain_b(n, 20)
                    dve.tensor_tensor(bd_k[:, :, :], bank[:, 0:TOPK].unsqueeze(1).to_broadcast([P, HEADS, TOPK]),
                                      mask.to_broadcast([P, HEADS, TOPK]), ALU.mult).then_inc(drained, 1)
                    bank, drained = drain_b(n, 21)
                    dve.tensor_tensor(bd_v[:, :, :], bank[:, 0:C].rearrange("p (h d) -> p h d", h=HEADS),
                                      mask.to_broadcast([P, HEADS, HD]), ALU.mult).then_inc(drained, 1)
                if s == AT_S2:
                    G = TILES * HEADS // 2
                    for h in range(2):
                        bank, drained = drain_b(n, 22 + h)
                        sc = bank[:, :].rearrange("p (g k) -> p g k", k=TOPK)
                        step(own, dve.tensor_reduce(m2[:, G * h:G * h + G], sc, AX.X, ALU.max))
                        ins = dve.tensor_tensor(E2[:, G * h:G * h + G, :], sc,
                                                m2[:, G * h:G * h + G].unsqueeze(2).to_broadcast([P, G, TOPK]), ALU.subtract)
                        ins.then_inc(drained, 1)
                if s == AT_E2:
                    G = TILES * HEADS // 2
                    dve.wait_ge(e2_exp, n + 1)
                    step(own, dve.tensor_reduce(den2[:, :], E2[:, :, :], AX.X, ALU.add))
                    step(own, dve.reciprocal(m2[:, :], den2[:, :]))
                    dve.tensor_tensor(E2[:, :, :], E2[:, :, :], m2[:, :].unsqueeze(2).to_broadcast([P, 2 * G, TOPK]),
                                      ALU.mult).then_inc(e2_ready, 1)
                if s == AT_TOK2:
                    for h in range(2):
                        bank, drained = drain_b(n, 26 + h)
                        dve.tensor_tensor(flat4(tok2, h), bank[:, :], flat4(tok, h), ALU.add).then_inc(drained, 1)
                        dve.wait_ge(drained, n * (AFTER // 2) + 14)
                    layer_norm(own, tok2, st1, ln1, LN1_EPS, after_done)
                    own[2] += 1
                    dve.wait_ge(own[0], own[1] + own[2])
                    for t in range(TILES):
                        ins = dve.tensor_scalar(that[:, t, :], tok2[:, t, :], ln1[:, 0, t:t + 1], ln1[:, 1, t:t + 1],
                                                ALU.subtract, ALU.mult)
                    ins.then_inc(that_ready, 1)
                if s in AT_FF:
                    f = AT_FF.index(s)
                    for h in range(2):
                        bank, drained = drain_b(n, 32 + 2 * f + h)
                        dve.tensor_scalar(hT[:, f, h * HALF:(h + 1) * HALF], bank[:, :], cols[:, 8 + f:9 + f], None, ALU.add)\
                            .then_inc(drained, 1)
                if s in AT_OUT:
                    h = AT_OUT.index(s)
                    if h == 0 and not (isinstance(n, int) and n == 0):
                        dve.wait_ge(out_done, 16 * n)
                    bank, drained = drain_b(n, 36 + h)
                    dve.tensor_tensor(tiles4(Y, h), bank[:, :].rearrange("p (t c) -> p t c", t=4),
                                      out_bias[:, :].unsqueeze(1).to_broadcast([P, 4, C]), ALU.add).then_inc(drained, 1)

            dve.memset(ones_row[:, :], 1.0)
            dve.memset(ones_col[:, :], 1.0)
            dve.memset(above[:, :], 0.0)
            dve.memset(no_maximum[:, :], 0.0)
            dve.memset(k_ones[:, :], 1.0).then_inc(vsetup, 1)
            dve.wait_ge(consts, 8)
            dve.tensor_copy(head_mask_b[:, :], head_mask[:, :])
            dve.tensor_copy(iota_f[:, :], iota_i[:, :]).then_inc(vsetup, 1)
            dve.wait_ge(weights_in, 16 * (WEIGHT_DMAS + 1))
            dve.tensor_copy(vecB[:, 0, :], BO.to_broadcast([P, C])).then_inc(vsetup, 1)
            dve.tensor_copy(vecB[:, 1, :], BF2.to_broadcast([P, C])).then_inc(vsetup, 1)
            dve.wait_ge(setup_filled, 1)
            dve.tensor_copy(wT[:, :, :].rearrange("p a c -> p (a c)"), A[:, 0:3 * P]).then_inc(vsetup, 1)
            dve.wait_ge(setup_filled, 2)
            dve.tensor_copy(wow[:, :], BC[0][:, 0:C]).then_inc(vsetup, 1)
            dve.tensor_copy(w2o[:, :, :].rearrange("p a c -> p (a c)"), BC[0][:, C:3 * C]).then_inc(vsetup, 1)
            dve.wait_ge(setup_filled, 3)
            dve.tensor_tensor(tok_bias[:, :], BC[1][:, 0:C], rows[:, 1, :], ALU.add).then_inc(vsetup, 1)
            dve.tensor_tensor(out_bias[:, :], BC[1][:, C:2 * C], rows[:, 2, :], ALU.add).then_inc(vsetup, 1)
            dve.wait_ge(vsetup, 9)

            turns = [0, 0]
            own = [before_done, 0, 0]
            for s in range(STEPS):
                before_tasks(0, turns, own, s)

            def image(n, base, first=False, last=False):
                dve.wait_ge(a_drained, base)
                dve.sem_inc(dve_passed, 1)
                with dve.If(dve.value_load(flag[0:1, 0:1], min_val=0, max_val=HEADS) > 0):
                    row_maxima(n)
                with dve.Else():
                    dve.sem_inc(max_drained, MAX_TILES)
                    dve.sem_inc(mneg_ready, 1)
                turns = [base, 0]
                own_b = [before_done, (n + 1) * BEFORE_STEPS, 0]
                own_a = [after_done, (n - 1) * AFTER_STEPS if not first else 0, 0]
                own_o = [att_done, n * PAIRS - (0 if first else 1), 0]
                for s in range(STEPS):
                    if s == 0 and not first:
                        copy_o(n - 1, PAIRS - 1)
                    if s > 0 and s % TILES == 0:
                        copy_o(n, s // TILES - 1)
                    if s == 1 and not first:
                        divide_o(n - 1, PAIRS - 1, turns, own_o)
                    if s > 1 and s % TILES == 1:
                        divide_o(n, s // TILES - 1, turns, own_o)
                    if not last:
                        before_tasks(n + 1, turns, own_b, s)
                    if not first:
                        after_tasks(n - 1, own_a, s)
                assert last or own_b[2] == BEFORE_STEPS
                assert first or own_a[2] == AFTER_STEPS

            image(0, FIRST_TURNS, first=True)
            with dve.Fori(1, IMAGES - 1) as n:
                image(n, FIRST_TURNS + TURNS_0 + (n - 1) * TURNS)
            base = FIRST_TURNS + TURNS_0 + (IMAGES - 2) * TURNS
            image(IMAGES - 1, base, last=True)
            copy_o(IMAGES - 1, PAIRS - 1)
            divide_o(IMAGES - 1, PAIRS - 1, [base + PAIRS, 0], [att_done, IMAGES * PAIRS - 1, 0])
            own = [after_done, (IMAGES - 1) * AFTER_STEPS, 0]
            for s in range(STEPS):
                after_tasks(IMAGES - 1, own, s)


_INS = ['x', 'L0_conv_ln_scale', 'L0_conv_ln_bias', 'L0_conv_w_qkv', 'L0_conv_b_qkv', 'L0_conv_w_out', 'L0_conv_b_out',
        'L1_conv_Win', 'L1_conv_b_in', 'L1_conv_Wq', 'L1_conv_Wk', 'L1_conv_Wv', 'L1_conv_g1', 'L1_conv_be1',
        'L1_conv_g2', 'L1_conv_be2', 'L1_conv_Wf1', 'L1_conv_bf1', 'L1_conv_Wf2', 'L1_conv_bf2', 'L1_conv_Wout',
        'L1_conv_bout']
_OUTS = [((8, 32, 32, 128), 'float32')]


def kernel(**inputs):
    import numpy as _np
    import concourse.bacc as _bacc
    from concourse import mybir as _mybir
    from concourse.bass_utils import run_bass_kernel_spmd as _run

    nc = _bacc.Bacc("TRN2", target_bir_lowering=False, num_devices=1)
    arrays, args = {}, []
    for name in _INS:
        a = _np.ascontiguousarray(inputs[name])
        arrays[f"in_{name}_dram"] = a
        args.append(nc.dram_tensor(f"in_{name}_dram", a.shape, _mybir.dt.from_np(a.dtype), kind="ExternalInput").ap())
    for i, (shape, dtype) in enumerate(_OUTS):
        dt = _mybir.dt.from_np(_np.dtype(dtype))
        args.append(nc.dram_tensor(f"out_{i}_dram", shape, dt, kind="ExternalOutput").ap())
    two_layers(nc, *args)
    r = _run(nc, [arrays], core_ids=[0])
    got = tuple(r.results[0][f"out_{i}_dram"] for i in range(len(_OUTS)))
    return got[0]
```

```python
import concourse.bass as bass
from concourse import mybir
from contextlib import ExitStack

P = 128
IMAGES, SIDE, C = 8, 32, 128
T = SIDE * SIDE
TILES = T // P
HALF = 512
HEADS, HD = 8, 16
PAIRS = HEADS // 2
PARTS = 3
ROWS1 = PARTS * 2 * HD
MROW = PARTS * HD
STEPS = PAIRS * TILES
POOL = 4
GRID = SIDE // POOL
POS = GRID * GRID
TOPK = 16
FF = 2 * C
SCALE = HD ** -0.5
SAFE_SQUARES = 60 / SCALE * 2 / 1.02
LN0_EPS, LN1_EPS = 1e-6, 1e-3
RSQRT_MAGIC = float(0x5F3759DF)

AT_LN0, AT_XN, AT_Q, AT_K, AT_V, AT_TOKX = 2, (8, 10), (11, 12), (13, 14), (15, 16), (18, 19)
AT_BOUND, AT_FLAG = (20, 21, 24, 26), 27
AT_AT, AT_TOK, AT_T, AT_Q1, AT_PK, AT_SC, AT_RT, AT_RB = 2, 4, 7, 7, 9, (11, 12, 13, 14), 15, 16
AT_SEL, AT_S2, AT_E2, AT_PT, AT_TOK2, AT_TT2, AT_T2 = 17, 18, 18, 20, 21, 23, 27
AT_FF, AT_GELU, AT_OUT = (28, 29), 29, (30, 31)

WARM = {AT_TOK: 4, AT_T: 28, AT_PK: 8, AT_SC[0]: 36, AT_SEL: 8, AT_PT: 16, AT_T2: 22, AT_OUT[0]: 8}
WAKE = 24

BEFORE = 15
AFTER = 38
TURNS_0 = PAIRS - 1 + BEFORE
TURNS = PAIRS + BEFORE
KQ_TURN = 6 + sum(TILES * j + 1 <= AT_K[1] for j in range(1, PAIRS))
V_TURN = 8 + sum(TILES * j + 1 <= AT_V[1] for j in range(1, PAIRS))
BEFORE_STEPS = 21
AFTER_STEPS = 45
FIRST_STEPS = 17


def two_layers(nc, x, ln_scale, ln_bias, w_qkv, b_qkv, w_out, b_out, Win, b_in, Wq, Wk, Wv, g1, be1, g2, be2,
               Wf1, bf1, Wf2, bf2, Wout, bout, out):
    fp32, f32r, bf16, i32 = mybir.dt.float32, mybir.dt.float32r, mybir.dt.bfloat16, mybir.dt.int32
    ALU = mybir.AluOpType
    ACT = mybir.ActivationFunctionType
    AX = mybir.AxisListType

    nc.disable_value_cache = True
    x_v = x.rearrange("n (t a) w c -> n (a w) t c", t=TILES)
    out_v = out.rearrange("n (t a) w c -> n (a w) t c", t=TILES)

    with ExitStack() as ctx:
        def sb(name, shape, dt=fp32):
            return ctx.enter_context(nc.sbuf_tensor(name, shape, dt))

        def sem(name):
            return ctx.enter_context(nc.semaphore(name))

        wqkv_s, wo_s, win_s = sb("wqkv_s", [P, 3 * C]), sb("wo_s", [P, C]), sb("win_s", [P, C])
        wq1_s, wkv1_s, wf1_s = sb("wq1_s", [P, C]), sb("wkv1_s", [P, 2 * C]), sb("wf1_s", [P, FF])
        wk3 = sb("wk3", [P, PAIRS, PARTS, 2 * HD])
        wf2_s, wout_s = sb("wf2_s", [P, 2, C]), sb("wout_s", [P, C])
        cols = sb("cols", [P, 12])
        LNS, LNB, BQ, BK, G1, BE1, G2, BE2, BO, BF2 = (cols[:, i:i + 1] for i in (0, 1, 2, 3, 4, 5, 6, 7, 10, 11))
        rows = sb("rows", [P, 3, C])
        wT = sb("wT", [P, 3, C])
        vecB = sb("vecB", [P, 2, C])
        wow = sb("wow", [P, C])
        w2o = sb("w2o", [P, 2, C])
        tok_bias, out_bias = sb("tok_bias", [P, C]), sb("out_bias", [P, C])
        win_sum, all_ones = sb("win_sum", [P, C]), sb("all_ones", [P, P])
        ident = sb("ident", [P, P])
        head_mask = sb("head_mask", [P, HEADS])
        below = sb("below", [POS, POS])
        iota_i, iota_f = sb("iota_i", [POS, TOPK], i32), sb("iota_f", [POS, TOPK])
        ones_row, ones_col = sb("ones_row", [1, POS]), sb("ones_col", [P, 1])
        X, xn = sb("X", [P, TILES, C]), sb("xn", [P, TILES, C])
        xhT, xnT = sb("xhT", [P, T]), sb("xnT", [P, T])
        squares, head_mask_b = sb("squares", [P, 2, T], bf16), sb("head_mask_b", [P, HEADS], bf16)
        peak, above, flag = sb("peak", [HEADS, 8]), sb("above", [P, 1]), sb("flag", [1, 1], i32)
        st0, ln0 = sb("st0", [P, TILES, 6]), sb("ln0", [P, 8, TILES])
        tokx_new, tokx = sb("tokx_new", [P, TILES, C]), sb("tokx", [P, TILES, C])
        qh, ql, kh, kl = (sb(n, [P, T], f32r) for n in ("qh", "ql", "kh", "kl"))
        v_new = sb("v_new", [P, TILES, C])
        Qs = sb("Qs", [P, PAIRS, T], f32r)
        Ks = sb("Ks", [P, HEADS, T], f32r)
        no_maximum = Ks[64:65, 0, :]
        Va = sb("Va", [P, TILES, HEADS, 32])
        Pr = sb("Pr", [P, 2, 2, T])
        mx, mneg = sb("mx", [P, HEADS * TILES]), sb("mneg", [HEADS * TILES, P], f32r)
        Ot, rden = sb("Ot", [P, HALF]), sb("rden", [P, 16])
        attn = sb("attn", [P, TILES, C])
        tok, tT, q1T = sb("tok", [P, TILES, C]), sb("tT", [P, T]), sb("q1T", [P, T])
        hT = sb("hT", [P, 2, T])
        st1, ln1 = sb("st1", [P, TILES, 6]), sb("ln1", [P, 8, TILES])
        pooled, pkv = sb("pooled", [P, POS]), sb("pkv", [POS, 2 * C])
        q1h, q1l = sb("q1h", [P, T], f32r), sb("q1l", [P, T], f32r)
        Q1s = sb("Q1s", [ROWS1, PAIRS, T], f32r)
        k1h, k1l = sb("k1h", [ROWS1, PAIRS, POS], f32r), sb("k1l", [ROWS1, PAIRS, POS], f32r)
        K1s = sb("K1s", [ROWS1, PAIRS, 2, POS], f32r)
        pair_mask = sb("pair_mask", [ROWS1, 2])
        r8, r1, rrow, red = sb("r8", [P, 8]), sb("r1", [P, 1]), sb("rrow", [1, P]), sb("red", [1, POS])
        rB, rsel, rcol = sb("rB", [POS, POS]), sb("rsel", [POS, POS]), sb("rcol", [POS, 1])
        rgt, rank, hot = sb("rgt", [POS, POS]), sb("rank", [POS, 1]), sb("hot", [POS, HEADS, TOPK])
        bd_k, bd_v = sb("bd_k", [P, HEADS, TOPK]), sb("bd_v", [P, HEADS, HD])
        m2, den2 = sb("m2", [P, TILES * HEADS]), sb("den2", [P, TILES * HEADS])
        E2, Y = sb("E2", [P, TILES * HEADS, TOPK]), sb("Y", [P, TILES, C])
        that, attnT = hT[:, 0, :].rearrange("p (t c) -> p t c", t=TILES), hT[:, 1, :]
        E2T, tok2T, tok2 = attnT, q1T, E2[:, :, :].rearrange("p (t g) k -> p t (g k)", t=TILES)
        k_ones = Y[0:1, :, :].rearrange("o t c -> o (t c)")

        S = ctx.enter_context(nc.psum_tensor("S", [P, 2, T], fp32))
        O = ctx.enter_context(nc.psum_tensor("O", [P, HALF], fp32))
        A = ctx.enter_context(nc.psum_tensor("A", [P, HALF], fp32))
        BC = [ctx.enter_context(nc.psum_tensor(f"BC{i}", [P, HALF], fp32)) for i in range(2)]

        qkv_in, fold_in, weights_in = sem("qkv_in"), sem("fold_in"), sem("weights_in")
        first_filled = sem("first_filled")
        first_act, first_dve = sem("first_act"), sem("first_dve")
        first_steps = sem("first_steps")
        consts = sem("consts")
        vsetup = sem("vsetup")
        folded = sem("folded")
        fold_copied, fold_added = sem("fold_copied"), sem("fold_added")
        half_xn = sem("half_xn")
        first_hi = sem("first_hi")
        x_in = sem("x_in")
        a_filled, a_drained = sem("a_filled"), sem("a_drained")
        b_filled = [sem("b_filled"), sem("c_filled")]
        b_drained = [sem("b_drained"), sem("c_drained")]
        ln0_ready, xn_ready, that_ready = sem("ln0_ready"), sem("xn_ready"), sem("that_ready")
        before_done = sem("before_done")
        att_done = sem("att_done")
        after_done = sem("after_done")
        squares_first, squares_ready = sem("squares_first"), sem("squares_ready")
        tokx_moved = sem("tokx_moved")
        means_ready = sem("means_ready")
        va_ready = sem("va_ready")
        stack_in = [sem(f"stack_in{j}") for j in range(PAIRS)]
        mrow_in = sem("mrow_in")
        max_filled, max_drained, mneg_ready, max_turned = sem("max_filled"), sem("max_drained"), sem("mneg_ready"), sem("max_turned")
        scores_ready, probs_ready, pv_done, o_copied = sem("scores_ready"), sem("probs_ready"), sem("pv_done"), sem("o_copied")
        e2_exp, e2_ready, gelu_ready = sem("e2_exp"), sem("e2_ready"), sem("gelu_ready")
        q1l_ready, q1_stacked = sem("q1l_ready"), sem("q1_stacked")
        pooled_ready, hot_ready = sem("pooled_ready"), sem("hot_ready")
        out_done = sem("out_done")
        sp_passed, pool_passed, pe_passed, dve_passed = sem("sp_passed"), sem("pool_passed"), sem("pe_passed"), sem("dve_passed")

        STACK_DMAS = 2 * (2 * PARTS + 1)
        MAX_TILES = HEADS * TILES
        QKV_DMAS, FOLD_DMAS, WEIGHT_DMAS = 6, 8, 10 + PARTS
        STACK1_DMAS = PAIRS * PARTS
        FIRST_FLAG, FIRST_DVE = 11, 13
        FIRST = [A, O, BC[0], BC[1], S[:, 0, 0:HALF], S[:, 0, HALF:T], S[:, 1, 0:HALF], S[:, 1, HALF:T]]

        def next_turn(turns):
            turns[1] += 1
            return turns[0] + turns[1]

        def half(t, h):
            return t[:, h * HALF:(h + 1) * HALF]

        def tiles4(t, h):
            return t[:, 4 * h:4 * h + 4, :]

        def flat4(t, h):
            return tiles4(t, h).rearrange("p a c -> p (a c)")

        def wait_for_flag(eng, base):
            if isinstance(base, int) and base == 0:
                eng.wait_ge(first_dve, FIRST_FLAG)
            else:
                eng.wait_ge(a_drained, base)

        block = ctx.enter_context(nc.Block())

        @block.sync
        def _(sp):
            def load_x(n):
                if not (isinstance(n, int) and n == 0):
                    sp.wait_ge(xn_ready, n)
                src = x_v[n] if isinstance(n, int) else x_v[bass.ds(n, 1)].rearrange("o p t c -> (o p) t c")
                sp.dma_start(X[:, :, :], src).then_inc(x_in, 16)

            def stack(n, j, drained, q_turns, k_turns):
                if not (isinstance(n, int) and n == 0):
                    sp.wait_ge(scores_ready, 2 * STEPS * (n - 1) + 2 * TILES * (j + 1))
                for a in range(2):
                    d = 64 * a + MROW
                    sp.dma_start(Qs[d:d + 1, j, :].bitcast(fp32), no_maximum.bitcast(fp32)).then_inc(stack_in[j], 16)
                sp.wait_ge(drained, q_turns)
                for a in range(2):
                    r = HD * (2 * j + a)
                    for part, q in enumerate((qh, qh, ql)):
                        d = 64 * a + HD * part
                        sp.dma_start(Qs[d:d + HD, j, :].bitcast(fp32), q[r:r + HD, :].bitcast(fp32)).then_inc(stack_in[j], 16)
                sp.wait_ge(drained, k_turns)
                for a in range(2):
                    r = HD * (2 * j + a)
                    for part, k in enumerate((kh, kl, kh)):
                        d = 64 * a + HD * part
                        sp.dma_start(Ks[d:d + HD, 2 * j + a, :].bitcast(fp32), k[r:r + HD, :].bitcast(fp32)).then_inc(stack_in[j], 16)

            def row_maximum(n):
                sp.wait_ge(mneg_ready, n + 1)
                for h in range(HEADS):
                    r = 64 * (h % 2) + MROW
                    sp.dma_start(Qs[r:r + 1, h // 2, :].rearrange("o (t q) -> o t q", t=TILES).bitcast(fp32),
                                 mneg[h * TILES:(h + 1) * TILES, :].bitcast(fp32)).then_inc(mrow_in, 16)

            def stack1(n):
                for part, q in enumerate((q1h, q1h, q1l)):
                    if part == 0:
                        for h in range(2):
                            sp.wait_ge(b_drained[h], n * (AFTER // 2) + 4)
                    if part == 2:
                        sp.wait_ge(q1l_ready, n + 1)
                    for j in range(PAIRS):
                        r = 2 * HD * j
                        sp.dma_start(Q1s[2 * HD * part:2 * HD * (part + 1), j, :].bitcast(fp32), q[r:r + 2 * HD, :].bitcast(fp32))\
                            .then_inc(q1_stacked, 16)

            def store(n):
                dst = out_v[n] if isinstance(n, int) else out_v[bass.ds(n, 1)].rearrange("o p t c -> (o p) t c")
                for h in range(2):
                    sp.wait_ge(b_drained[h], (n + 1) * (AFTER // 2))
                    sp.dma_start(dst[:, 4 * h:4 * h + 4, :], tiles4(Y, h)).then_inc(out_done, 16)

            col = lambda v, s: v[s:s + C].rearrange("(p o) -> p o", o=1)
            load_x(0)
            for group, loads in (
                    (qkv_in, ((LNS, col(ln_scale, 0)), (LNB, col(ln_bias, 0)), (wqkv_s[:, :], w_qkv), (BQ, col(b_qkv, 0)),
                              (BK, col(b_qkv, C)), (rows[:, 0, :], b_qkv[2 * C:3 * C].partition_broadcast(P)))),
                    (fold_in, ((wo_s[:, :], w_out), (wf2_s[:, :, :], Wf2.rearrange("(a p) c -> p a c", a=2)),
                               (win_s[:, :], Win), (wout_s[:, :], Wout), (BO, col(b_out, 0)), (BF2, col(bf2, 0)),
                               (rows[:, 1, :], b_in.partition_broadcast(P)), (rows[:, 2, :], bout.partition_broadcast(P))))):
                for dst, src in loads:
                    sp.dma_start(dst, src).then_inc(group, 16)
            sp.wait_ge(consts, 12)
            sp.wait_ge(vsetup, 1)

            def key_ones(j):
                for h in (2 * j, 2 * j + 1):
                    r = 64 * (h % 2) + MROW
                    sp.dma_start(Ks[r:r + 1, h, :].bitcast(fp32), k_ones[:, :]).then_inc(stack_in[j], 16)

            key_ones(0)
            stack(0, 0, first_dve, 2, 4)
            load_x(1)
            for j in range(1, PAIRS):
                key_ones(j)
                stack(0, j, first_dve, 2, 4)
            for dst, src in ((wq1_s[:, :], Wq), (wkv1_s[:, 0:C], Wk), (wkv1_s[:, C:2 * C], Wv), (wf1_s[:, :], Wf1),
                             (G1, col(g1, 0)), (BE1, col(be1, 0)), (G2, col(g2, 0)), (BE2, col(be2, 0)),
                             (cols[:, 8:9], col(bf1, 0)), (cols[:, 9:10], col(bf1, C)),
                             *((wk3[:, :, i, :], Wk.rearrange("c (j e) -> c j e", j=PAIRS)) for i in range(PARTS))):
                sp.dma_start(dst, src).then_inc(weights_in, 16)

            def image(n, base, first=False, last=False, load=True):
                wait_for_flag(sp, base)
                sp.sem_inc(sp_passed, 1)
                with sp.If(sp.value_load(flag[0:1, 0:1], min_val=0, max_val=HEADS) > 0):
                    row_maximum(n)
                with sp.Else():
                    sp.sem_inc(mrow_in, 16 * HEADS)
                k_turn = base + (0 if first else 1) + KQ_TURN
                if load and not last:
                    load_x(n + 2)
                if not first:
                    stack1(n - 1)
                if not last:
                    for j in range(PAIRS - 1):
                        stack(n + 1, j, a_drained, k_turn - 2, k_turn)
                if not first:
                    store(n - 1)
                if not last:
                    stack(n + 1, PAIRS - 1, a_drained, k_turn - 2, k_turn)

            image(0, 0, first=True)
            with sp.Fori(1, IMAGES - 2) as n:
                image(n, TURNS_0 + (n - 1) * TURNS)
            image(IMAGES - 2, TURNS_0 + (IMAGES - 3) * TURNS, load=False)
            image(IMAGES - 1, TURNS_0 + (IMAGES - 2) * TURNS, last=True)
            stack1(IMAGES - 1)
            store(IMAGES - 1)
            sp.wait_ge(out_done, 2 * 16 * IMAGES)

        @block.gpsimd
        def _(pool):
            def wait(signal, value):
                pool.wait_ge(signal, value)
                pool.sem_inc(pool_passed, 1)

            def step(n, ins):
                ins.then_inc(consts, 1)
                pool.wait_ge(consts, n)

            step(1, pool.memset(ident[:, :], 0.0))
            step(2, pool.affine_select(out=ident[:, :], in_=ident[:, :], compare_op=ALU.not_equal, fill=1.0, base=0,
                                       pattern=[[-1, P]], channel_multiplier=1))
            step(3, pool.memset(head_mask[:, :], 1.0))
            step(4, pool.affine_select(out=head_mask[:, :], in_=head_mask[:, :], compare_op=ALU.is_ge, fill=0.0, base=0,
                                       pattern=[[-HD, HEADS]], channel_multiplier=1))
            step(5, pool.affine_select(out=head_mask[:, :], in_=head_mask[:, :], compare_op=ALU.is_ge, fill=0.0,
                                       base=HD - 1, pattern=[[HD, HEADS]], channel_multiplier=-1))
            step(6, pool.memset(below[:, :], 1.0))
            step(7, pool.affine_select(out=below[:, :], in_=below[:, :], compare_op=ALU.is_gt, fill=0.0, base=0,
                                       pattern=[[-1, POS]], channel_multiplier=1))
            for i in range(PARTS):
                step(8 + i, pool.tensor_copy(pair_mask[2 * HD * i:2 * HD * (i + 1), :], head_mask[0:2 * HD, 0:2]))
            step(11, pool.iota(iota_i[:, :], pattern=[[1, TOPK]], base=0, channel_multiplier=0))
            pool.memset(Ks[:, :, :].bitcast(fp32), 0.0)
            step(12, pool.memset(Qs[:, :, :].bitcast(fp32), 0.0))
            step(13, pool.memset(Va[:, :, :, :], 1.0))

            def normalise(dst, src, ln, ready, need, done):
                wait(ready, need)
                for t in range(TILES):
                    ins = pool.tensor_scalar(dst[:, t, :], src[:, t, :], ln[:, 0, t:t + 1], ln[:, 1, t:t + 1],
                                             ALU.subtract, ALU.mult)
                ins.then_inc(done, 1)

            def place_v(n, j, v_drained, turns):
                wait(v_drained, turns)
                if not (isinstance(n, int) and n == 0):
                    wait(pv_done, STEPS * (n - 1) + TILES * (j + 1))
                pool.tensor_copy(Va[:, :, 2 * j:2 * j + 2, 0:HD],
                                 v_new[:, :, 2 * HD * j:2 * HD * (j + 1)].rearrange("p t (h d) -> p t h d", h=2))\
                    .then_inc(va_ready, 1)

            def means_share(n):
                wait(fold_added, 3)
                wait(ln0_ready, n + 1)
                if not (isinstance(n, int) and n == 0):
                    wait(tokx_moved, n)
                for t in range(TILES):
                    ins = pool.tensor_scalar(tokx_new[:, t, :], win_sum[:, :], ln0[:, 0, t:t + 1], None, ALU.mult)
                ins.then_inc(means_ready, 1)

            def square(n, k_turn):
                wait(a_drained, k_turn)
                for i, part in enumerate((qh, kh)):
                    ins = pool.tensor_tensor(squares[:, i, :], part[:, :].bitcast(fp32), part[:, :].bitcast(fp32), ALU.mult)
                ins.then_inc(squares_ready, 1)

            def q1_rest(n):
                wait(b_drained[0], n * (AFTER // 2) + 4)
                wait(b_drained[1], n * (AFTER // 2) + 4)
                if not (isinstance(n, int) and n == 0):
                    wait(q1_stacked, 16 * STACK1_DMAS * n)
                pool.tensor_tensor(q1l[:, :], q1T[:, :], q1h[:, :].bitcast(fp32), ALU.subtract).then_inc(q1l_ready, 1)

            for j in range(PAIRS):
                place_v(0, j, first_dve, 6)
            means_share(0)

            def image(n, base, first=False, last=False):
                v_turn = base + (0 if first else 1) + V_TURN
                if not first:
                    place_v(n, PAIRS - 1, a_drained, base)
                    wait(b_drained[1], (n - 1) * (AFTER // 2) + 2)
                if first:
                    wait(first_dve, FIRST_DVE)
                else:
                    wait(a_drained, base)
                pool.tensor_tensor(tokx[:, :, :], tokx_new[:, :, :], tok_bias[:, :].unsqueeze(1).to_broadcast([P, TILES, C]),
                                   ALU.add).then_inc(tokx_moved, 1)
                if not last:
                    normalise(xn, X, ln0, ln0_ready, n + 2, xn_ready)
                if not first:
                    q1_rest(n - 1)
                if not last:
                    square(n + 1, v_turn - V_TURN + KQ_TURN)
                    means_share(n + 1)
                    place_v(n + 1, 0, a_drained, v_turn)
                    place_v(n + 1, 1, a_drained, v_turn)
                    place_v(n + 1, 2, a_drained, v_turn)

            image(0, 0, first=True)
            with pool.Fori(1, IMAGES - 1) as n:
                image(n, TURNS_0 + (n - 1) * TURNS)
            image(IMAGES - 1, TURNS_0 + (IMAGES - 2) * TURNS, last=True)
            q1_rest(IMAGES - 1)

        @block.tensor
        def _(pe):
            def b_turn(n, k):
                b, before = k % 2, n * (AFTER // 2) + k // 2
                if not (isinstance(before, int) and before == 0):
                    pe.wait_ge(b_drained[b], before)
                return BC[b], b_filled[b]

            def b_ready(n, k):
                pe.wait_ge(b_drained[k % 2], n * (AFTER // 2) + k // 2 + 1)

            def a_turn(turns):
                k = next_turn(turns)
                if not (isinstance(k, int) and k == 1):
                    pe.wait_ge(a_drained, k - 1)

            def before_tasks(n, turns, s):
                if s in AT_XN:
                    h = AT_XN.index(s)
                    pe.wait_ge(xn_ready, n + 1)
                    a_turn(turns)
                    for t in range(4):
                        mm = pe.transpose(A[:, t * P:(t + 1) * P], xn[:, 4 * h + t, :], ident[:, :])
                    mm.then_inc(a_filled, 1)
                if s in AT_Q + AT_K:
                    c, h = (0, AT_Q.index(s)) if s in AT_Q else (C, AT_K.index(s))
                    a_turn(turns)
                    pe.matmul(A[:, :], wqkv_s[:, c:c + C], half(xnT, h), start=True, stop=True).then_inc(a_filled, 1)
                if s in AT_V:
                    a_turn(turns)
                    by_token(A, a_filled, [(xnT, wqkv_s[:, 2 * C:3 * C])], AT_V.index(s))
                if s in AT_TOKX:
                    a_turn(turns)
                    by_token(A, a_filled, [(xhT, win_s[:, :])], AT_TOKX.index(s))
                if s in AT_BOUND:
                    i, h = divmod(AT_BOUND.index(s), 2)
                    pe.wait_ge(squares_ready, n)
                    a_turn(turns)
                    pe.matmul(A[0:HEADS, :], head_mask_b[:, :], squares[:, i, h * HALF:(h + 1) * HALF],
                              start=True, stop=True).then_inc(a_filled, 1)
                if s == AT_FLAG:
                    pe.wait_ge(before_done, n * BEFORE_STEPS)
                    a_turn(turns)
                    pe.matmul(A[0:1, 0:1], above[:, :], ones_col[:, :], start=True, stop=True).then_inc(a_filled, 1)

            def row_maxima(n):
                for j in range(PAIRS):
                    pe.wait_ge(stack_in[j], 32 + 16 * STACK_DMAS * (n + 1))
                if not (isinstance(n, int) and n == 0):
                    pe.wait_ge(probs_ready, 2 * STEPS * n)
                for t in range(TILES):
                    for h in range(HEADS):
                        k = t * HEADS + h
                        if not (isinstance(n, int) and n == 0 and k < 2):
                            pe.wait_ge(max_drained, MAX_TILES * n + k - 1)
                        r = 64 * (h % 2)
                        for c in range(2):
                            mm = pe.matmul(S[:, k % 2, c * HALF:(c + 1) * HALF],
                                           Qs[r:r + MROW, h // 2, t * P:(t + 1) * P],
                                           Ks[r:r + MROW, h, c * HALF:(c + 1) * HALF], start=True, stop=True)
                        mm.then_inc(max_filled, 1)
                pe.wait_ge(max_drained, MAX_TILES * (n + 1))
                pe.sem_inc(pe_passed, 1)
                pe.transpose(S[0:MAX_TILES, 0, 0:P], mx[:, :], ident[:, :]).then_inc(max_turned, 1)
                pe.wait_ge(mneg_ready, n + 1)
                pe.wait_ge(mrow_in, 16 * HEADS * (n + 1))

            def scores(n, s, a):
                j, kb = s // TILES, s % TILES
                before = 2 * STEPS * n + 2 * s + a - 1
                if not (isinstance(before, int) and before <= 0):
                    pe.wait_ge(probs_ready, before)
                if kb == 0 and a == 0:
                    pe.wait_ge(stack_in[j], 32 + 16 * STACK_DMAS * (n + 1))
                for c in range(2):
                    mm = pe.matmul(S[:, a, c * HALF:(c + 1) * HALF], Ks[:, 2 * j + a, kb * P:(kb + 1) * P],
                                   Qs[:, j, c * HALF:(c + 1) * HALF], start=True, stop=True)
                mm.then_inc(scores_ready, 1)

            def weighted(n, s):
                j, kb = s // TILES, s % TILES
                pe.wait_ge(probs_ready, 2 * STEPS * n + 2 * s + 2)
                if kb == 0:
                    pe.wait_ge(va_ready, PAIRS * n + j + 1)
                    if not (isinstance(n, int) and n == 0 and j == 0):
                        pe.wait_ge(o_copied, PAIRS * n + j)
                for a in range(2):
                    for c in range(2):
                        r = 32 * (2 * a + c)
                        mm = pe.matmul(O[r:r + 32, :], Va[:, kb, 2 * j + a, :], Pr[:, s % 2, a, c * HALF:(c + 1) * HALF],
                                       start=(kb == 0), stop=(kb == TILES - 1))
                mm.then_inc(pv_done, 1)

            def turn_o(n, j, turns):
                pe.wait_ge(o_copied, PAIRS * n + j + 1)
                a_turn(turns)
                for t in range(4):
                    mm = pe.transpose(A[:, t * P:(t + 1) * P], Ot[:, t * P:(t + 1) * P], ident[:, :])
                mm.then_inc(a_filled, 1)

            def turn4(bank, filled, src, h):
                for t in range(4):
                    mm = pe.transpose(bank[:, t * P:(t + 1) * P], src[:, 4 * h + t, :], ident[:, :])
                mm.then_inc(filled, 1)

            def by_token(bank, filled, pairs, h):
                for t in range(4):
                    c = (4 * h + t) * P
                    for i, (lhs, w) in enumerate(pairs):
                        mm = pe.matmul(bank[:, t * P:(t + 1) * P], lhs[:, c:c + P], w, start=(i == 0),
                                       stop=(i == len(pairs) - 1))
                mm.then_inc(filled, 1)

            def after_tasks(n, s, attn_turn):
                if s == AT_AT:
                    pe.wait_ge(a_drained, attn_turn)
                    for h in range(2):
                        turn4(*b_turn(n, h), attn, h)
                if s == AT_TOK:
                    for h in range(2):
                        b_ready(n, h)
                        by_token(*b_turn(n, 2 + h), [(attnT, wow[:, :])], h)
                if s == AT_T:
                    for h in range(2):
                        pe.wait_ge(that_ready, 4 * n + 1 + h)
                        turn4(*b_turn(n, 4 + h), that, h)
                if s == AT_Q1:
                    for h in range(2):
                        b_ready(n, 4 + h)
                        bank, filled = b_turn(n, 6 + h)
                        pe.matmul(bank[:, :], wq1_s[:, :], half(tT, h), start=True, stop=True).then_inc(filled, 1)
                if s == AT_PK:
                    pe.wait_ge(pooled_ready, 2 * n + 2)
                    bank, filled = b_turn(n, 8)
                    for j in range(PAIRS):
                        mm = pe.matmul(bank[0:ROWS1, j * POS:(j + 1) * POS], wk3[:, j, :, :].rearrange("p a b -> p (a b)"),
                                       pooled[:, :], start=True, stop=True)
                    mm.then_inc(filled, 1)
                    bank, filled = b_turn(n, 9)
                    pe.matmul(bank[0:POS, 0:2 * C], pooled[:, :], wkv1_s[:, :], start=True, stop=True).then_inc(filled, 1)
                for j in range(PAIRS):
                    if s != AT_SC[j]:
                        continue
                    if j == 0:
                        b_ready(n, 8)
                        pe.wait_ge(q1_stacked, 16 * STACK1_DMAS * (n + 1))
                    for h in range(2):
                        bank, filled = b_turn(n, 10 + 2 * j + h)
                        pe.matmul(bank[:, :], K1s[:, j, :, :].rearrange("p a b -> p (a b)"), half(Q1s[:, j, :], h),
                                  start=True, stop=True).then_inc(filled, 1)
                if s == AT_RT:
                    b_ready(n, 17)
                    bank, filled = b_turn(n, 18)
                    pe.sem_inc(pe_passed, 1)
                    pe.transpose(bank[0:1, 0:P], r1[:, :], ident[:, :]).then_inc(filled, 1)
                if s == AT_RB:
                    b_ready(n, 18)
                    bank, filled = b_turn(n, 19)
                    pe.matmul(bank[0:POS, 0:POS], ones_row[:, :], red[:, :], start=True, stop=True).then_inc(filled, 1)
                if s == AT_SEL:
                    pe.wait_ge(hot_ready, n + 1)
                    bank, filled = b_turn(n, 20)
                    pe.matmul(bank[:, 0:TOPK], pkv[:, 0:C], hot[:, 0, :], start=True, stop=True).then_inc(filled, 1)
                    bank, filled = b_turn(n, 21)
                    pe.matmul(bank[:, 0:C], hot[:, :, :].rearrange("p a b -> p (a b)"), pkv[:, C:2 * C],
                              start=True, stop=True).then_inc(filled, 1)
                if s == AT_S2:
                    b_ready(n, 6)
                    b_ready(n, 7)
                    b_ready(n, 20)
                    for h in range(2):
                        by_token(*b_turn(n, 22 + h), [(q1T, bd_k[:, :, :].rearrange("p a b -> p (a b)"))], h)
                if s == AT_PT:
                    for h in range(2):
                        pe.wait_ge(e2_ready, 2 * n + 1 + h)
                        turn4(*b_turn(n, 24 + h), E2[:, :, :].rearrange("p (t h) k -> p t (h k)", t=TILES), h)
                if s == AT_TOK2:
                    for h in range(2):
                        b_ready(n, 24 + h)
                        by_token(*b_turn(n, 26 + h), [(E2T, bd_v[:, :, :].rearrange("p a b -> p (a b)"))], h)
                if s == AT_TT2:
                    for h in range(2):
                        b_ready(n, 26 + h)
                        turn4(*b_turn(n, 28 + h), tok2, h)
                if s == AT_T2:
                    for h in range(2):
                        pe.wait_ge(that_ready, 4 * n + 3 + h)
                        turn4(*b_turn(n, 30 + h), that, h)
                if s in AT_FF:
                    f = AT_FF.index(s)
                    for h in range(2):
                        b_ready(n, 30 + h)
                        bank, filled = b_turn(n, 32 + 2 * f + h)
                        pe.matmul(bank[:, :], wf1_s[:, f * C:(f + 1) * C], half(tT, h), start=True, stop=True)\
                            .then_inc(filled, 1)
                if s == AT_GELU:
                    for h in range(2):
                        bank, filled = b_turn(n, 36 + h)
                        for t in range(4):
                            c = (4 * h + t) * P
                            pe.matmul(bank[:, t * P:(t + 1) * P], tok2T[:, c:c + P], wout_s[:, :],
                                      start=(t == 0), stop=False)
                if s in AT_OUT:
                    h = AT_OUT.index(s)
                    for f in range(2):
                        pe.wait_ge(gelu_ready, 2 * n + 1 + f)
                        for t in range(4):
                            c = (4 * h + t) * P
                            mm = pe.matmul(BC[h][:, t * P:(t + 1) * P], hT[:, f, c:c + P], w2o[:, f, :],
                                           start=False, stop=(t == 3 and f == 1))
                    mm.then_inc(b_filled[h], 1)

            def by_token_first(bank, lhs, w, h):
                by_token(bank, first_filled, [(lhs, w)], h)

            pe.wait_ge(consts, 2)
            for _ in range(WAKE):
                pe.matmul(FIRST[4][:, 0:P], ident[:, :], ident[:, :], start=True, stop=True)
            for h in range(2):
                pe.wait_ge(xn_ready if h else half_xn, 1)
                turn4(FIRST[6 + h], first_filled, xn, h)
            pe.wait_ge(qkv_in, 16 * QKV_DMAS)
            for i in range(4):
                if i < 2:
                    pe.wait_ge(first_act, 1 + i)
                pe.matmul(FIRST[4 + i], wqkv_s[:, i // 2 * C:(i // 2 + 1) * C], half(xnT, i % 2), start=True, stop=True)\
                    .then_inc(first_filled, 1)
            pe.wait_ge(fold_in, 16 * FOLD_DMAS)
            pe.transpose(BC[0][:, 0:P], wo_s[:, :], ident[:, :])
            pe.transpose(BC[0][:, P:2 * P], wf2_s[:, 0, :], ident[:, :])
            pe.transpose(BC[0][:, 2 * P:3 * P], wf2_s[:, 1, :], ident[:, :]).then_inc(folded, 1)
            for h in range(2):
                by_token_first(FIRST[h], xnT, wqkv_s[:, 2 * C:3 * C], h)
            pe.wait_ge(fold_copied, 2)
            pe.matmul(BC[1][:, 0:C], wT[:, 0, :], win_s[:, :], start=True, stop=True)
            pe.matmul(BC[1][:, C:2 * C], wT[:, 1, :], wout_s[:, :], start=True, stop=True)
            pe.matmul(BC[1][:, 2 * C:3 * C], wT[:, 2, :], wout_s[:, :], start=True, stop=True).then_inc(folded, 1)
            pe.matmul(BC[0][:, 0:C], vecB[:, 0, :], win_s[:, :], start=True, stop=True)
            pe.matmul(BC[0][:, C:2 * C], vecB[:, 1, :], wout_s[:, :], start=True, stop=True)
            pe.wait_ge(vsetup, 1)
            pe.matmul(BC[0][:, 2 * C:3 * C], all_ones[:, :], win_s[:, :], start=True, stop=True).then_inc(folded, 1)
            pe.wait_ge(vsetup, 2)
            for i in range(4):
                pe.wait_ge(squares_first, 1 + i // 2)
                pe.matmul(FIRST[4 + i][0:HEADS, :], head_mask_b[:, :], squares[:, i // 2, i % 2 * HALF:(i % 2 + 1) * HALF],
                          start=True, stop=True).then_inc(first_filled, 1)
            pe.wait_ge(first_dve, 10)
            pe.wait_ge(first_steps, FIRST_STEPS)
            pe.matmul(FIRST[4][0:1, 0:1], above[:, :], ones_col[:, :], start=True, stop=True).then_inc(first_filled, 1)
            pe.wait_ge(fold_added, 3)
            pe.wait_ge(fold_copied, 3)
            for h in range(2):
                by_token_first(BC[h], xhT, win_s[:, :], h)

            def image(n, base, first=False, last=False):
                wait_for_flag(pe, base)
                pe.sem_inc(pe_passed, 1)
                with pe.If(pe.value_load(flag[0:1, 0:1], min_val=0, max_val=HEADS) > 0):
                    row_maxima(n)
                with pe.Else():
                    pe.sem_inc(max_filled, MAX_TILES)
                    pe.sem_inc(max_turned, 1)
                turns = [base, 0]
                for s in range(STEPS):
                    scores(n, s, 0)
                    scores(n, s, 1)
                    if s > 0:
                        weighted(n, s - 1)
                    elif not first:
                        weighted(n - 1, STEPS - 1)
                    if s == 1 and not first:
                        turn_o(n - 1, PAIRS - 1, turns)
                    if s > 1 and s % TILES == 1:
                        turn_o(n, s // TILES - 1, turns)
                    if not last:
                        before_tasks(n + 1, turns, s)
                    if not first:
                        after_tasks(n - 1, s, base + 1)

            image(0, 0, first=True)
            pe.wait_ge(weights_in, 16 * WEIGHT_DMAS)
            pe.wait_ge(first_dve, FIRST_DVE)
            with pe.Fori(1, IMAGES - 1) as n:
                image(n, TURNS_0 + (n - 1) * TURNS)
            base = TURNS_0 + (IMAGES - 2) * TURNS
            image(IMAGES - 1, base, last=True)
            weighted(IMAGES - 1, STEPS - 1)
            turn_o(IMAGES - 1, PAIRS - 1, [base + PAIRS, 0])
            for s in range(STEPS):
                for _ in range(WARM.get(s, 0)):
                    pe.matmul(S[:, 0, 0:HALF], Ks[:, 0, 0:P], Qs[:, 0, 0:HALF], start=True, stop=True)
                after_tasks(IMAGES - 1, s, base + PAIRS + 1)

        @block.scalar
        def _(act):
            def drain_a(turns):
                k = next_turn(turns)
                act.wait_ge(a_filled, k)

            def drain_b(n, k):
                act.wait_ge(b_filled[k % 2], n * (AFTER // 2) + k // 2 + 1)
                return BC[k % 2], b_drained[k % 2]

            def exps(n, s, a):
                act.wait_ge(scores_ready, 2 * STEPS * n + 2 * s + a + 1)
                used = STEPS * n + s - 1
                if a == 0 and not (isinstance(used, int) and used <= 0):
                    act.wait_ge(pv_done, used)
                act.activation(Pr[:, s % 2, a, :], S[:, a, :], ACT.Exp, scale=SCALE).then_inc(probs_ready, 1)

            def before_tasks(n, turns, s):
                if s in AT_XN:
                    h = AT_XN.index(s)
                    drain_a(turns)
                    act.activation(half(xhT, h), A[:, :], ACT.Copy)
                    act.activation(half(xnT, h), A[:, :], ACT.Identity, bias=LNB, scale=LNS).then_inc(a_drained, 1)
                for _ in range((AT_Q + AT_K + AT_V + AT_TOKX + AT_BOUND + (AT_FLAG,)).count(s)):
                    next_turn(turns)

            def after_tasks(n, s):
                if s in (AT_T, AT_T2):
                    g, be, k0 = (G1, BE1, 4) if s == AT_T else (G2, BE2, 30)
                    for h in range(2):
                        bank, drained = drain_b(n, k0 + h)
                        act.activation(half(tT, h), bank[:, :], ACT.Identity, bias=be, scale=g).then_inc(drained, 1)
                if s == AT_Q1:
                    if not (isinstance(n, int) and n == 0):
                        act.wait_ge(q1_stacked, 16 * STACK1_DMAS * n)
                    for h in range(2):
                        bank, drained = drain_b(n, 6 + h)
                        act.activation(half(q1T, h), bank[:, :], ACT.Copy)
                        act.activation(half(q1h, h), bank[:, :], ACT.Copy).then_inc(drained, 1)
                if s in (AT_PT, AT_TT2):
                    dst, k0 = {AT_PT: (E2T, 24), AT_TT2: (tok2T, 28)}[s]
                    for h in range(2):
                        bank, drained = drain_b(n, k0 + h)
                        act.activation(half(dst, h), bank[:, :], ACT.Copy).then_inc(drained, 1)
                if s == AT_S2:
                    for h in range(2):
                        act.wait_ge(b_drained[h], n * (AFTER // 2) + 12)
                        g = slice(TILES * HEADS // 2 * h, TILES * HEADS // 2 * (h + 1))
                        act.activation(E2[:, g, :], E2[:, g, :], ACT.Exp, scale=SCALE).then_inc(e2_exp, 1)
                if s == AT_GELU:
                    for f in range(2):
                        for h in range(2):
                            act.wait_ge(b_drained[h], n * (AFTER // 2) + 17 + f)
                        act.activation(hT[:, f, :], hT[:, f, :], ACT.Gelu).then_inc(gelu_ready, 1)

            act.wait_ge(fold_in, 16 * FOLD_DMAS)
            act.wait_ge(consts, 2)
            act.activation(vecB[:, 0, :], ident[:, :], ACT.Identity, bias=BO, scale=0.0)
            act.activation(vecB[:, 1, :], ident[:, :], ACT.Identity, bias=BF2, scale=0.0).then_inc(fold_copied, 1)
            act.wait_ge(qkv_in, 16 * QKV_DMAS)
            for h in range(2):
                act.wait_ge(first_filled, 1 + h)
                act.activation(half(xnT, h), FIRST[6 + h][:, :], ACT.Identity, bias=LNB, scale=LNS)
                act.activation(half(xhT, h), FIRST[6 + h][:, :], ACT.Copy).then_inc(first_act, 1)
            for i in range(4):
                act.wait_ge(first_filled, 3 + i)
                act.activation(half(kh if i >= 2 else qh, i % 2), FIRST[4 + i][:, :], ACT.Identity, bias=BK if i >= 2 else BQ)\
                    .then_inc(first_hi, 1)
            act.wait_ge(folded, 1)
            act.activation(wT[:, :, :].rearrange("p a c -> p (a c)"), BC[0][:, 0:3 * P], ACT.Copy).then_inc(fold_copied, 1)
            for i, part in enumerate((qh, kh)):
                if i == 1:
                    act.wait_ge(folded, 2)
                    act.activation(wow[:, :], BC[1][:, 0:C], ACT.Copy)
                    act.activation(w2o[:, :, :].rearrange("p a c -> p (a c)"), BC[1][:, C:3 * C], ACT.Copy).then_inc(fold_copied, 1)
                act.wait_ge(first_hi, 2 + 2 * i)
                act.wait_ge(first_dve, 2 + 2 * i)
                act.activation(squares[:, i, :], part[:, :].bitcast(fp32), ACT.Square).then_inc(squares_first, 1)

            def image(n, base, first=False, last=False):
                turns = [base, 0]
                for s in range(STEPS):
                    exps(n, s, 0)
                    exps(n, s, 1)
                    if (s == 1 and not first) or (s > 1 and s % TILES == 1):
                        next_turn(turns)
                    if not last:
                        before_tasks(n + 1, turns, s)
                    if not first:
                        after_tasks(n - 1, s)

            image(0, 0, first=True)
            act.wait_ge(weights_in, 16 * WEIGHT_DMAS)
            with act.Fori(1, IMAGES - 1) as n:
                image(n, TURNS_0 + (n - 1) * TURNS)
            image(IMAGES - 1, 0, last=True)
            for s in range(STEPS):
                after_tasks(IMAGES - 1, s)

        @block.vector
        def _(dve):
            def step(own, ins):
                ins.then_inc(own[0], 1)
                own[2] += 1
                dve.wait_ge(own[0], own[1] + own[2])

            def drain_a(turns):
                dve.wait_ge(a_filled, next_turn(turns))

            def drain_b(n, k):
                dve.wait_ge(b_filled[k % 2], n * (AFTER // 2) + k // 2 + 1)
                return BC[k % 2], b_drained[k % 2]

            def layer_norm(own, src, st, ln, eps, ready, deviation=False):
                for t in range(TILES):
                    ins = dve.bn_stats(st[:, t, :], src[:, t, :])
                step(own, ins)
                m_e, v_e, m_o, v_o = (st[:, :, i] for i in (1, 2, 4, 5))
                mean, y, d, v, w, g = (ln[:, i, :] for i in range(6))
                dve.tensor_tensor(mean, m_e, m_o, ALU.add)
                dve.tensor_tensor(v, v_e, v_o, ALU.add)
                step(own, dve.tensor_tensor(d, m_e, m_o, ALU.subtract))
                dve.tensor_scalar(mean, mean, 0.5, None, ALU.mult)
                dve.tensor_scalar(v, v, 1.0 / C, eps, ALU.mult, ALU.add)
                step(own, dve.scalar_tensor_tensor(out=w, in0=d, scalar=0.25, in1=d, op0=ALU.mult, op1=ALU.mult))
                step(own, dve.tensor_tensor(v, v, w, ALU.add))
                dve.tensor_scalar(w, v, -0.5, None, ALU.mult)
                step(own, dve.tensor_scalar(y.bitcast(i32), v.bitcast(i32), -0.5, RSQRT_MAGIC, ALU.mult, ALU.add))
                for k in range(3):
                    step(own, dve.tensor_tensor(g, y, y, ALU.mult))
                    step(own, dve.tensor_tensor(d, g, w, ALU.mult))
                    ins = dve.scalar_tensor_tensor(out=y, in0=d, scalar=1.5, in1=y, op0=ALU.add, op1=ALU.mult)
                    if k < 2:
                        step(own, ins)
                if deviation:
                    step(own, ins)
                    ins = dve.tensor_tensor(ln[:, 6, :], v, y, ALU.mult)
                ins.then_inc(ready, 1)

            def drain_tokx(bank, h):
                for i in range(4):
                    t = 4 * h + i
                    ins = dve.scalar_tensor_tensor(out=tokx_new[:, t, :], in0=bank[:, i * C:(i + 1) * C],
                                                   scalar=ln0[:, 6, t:t + 1], in1=tokx_new[:, t, :], op0=ALU.mult, op1=ALU.add)
                return ins

            def drain_qk(own, bank, is_k, h):
                hi, lo, bias = (kh, kl, BK) if is_k else (qh, ql, BQ)
                step(own, dve.tensor_scalar(half(hi, h), bank, bias, None, ALU.add))
                return dve.scalar_tensor_tensor(out=half(lo, h), in0=bank, scalar=bias, in1=half(hi, h).bitcast(fp32),
                                                op0=ALU.add, op1=ALU.subtract)

            def drain_v(bank, h):
                return dve.tensor_tensor(tiles4(v_new, h), bank[:, :].rearrange("p (t c) -> p t c", t=4),
                                         rows[:, 0:1, :].to_broadcast([P, 4, C]), ALU.add)

            def bound(own):
                step(own, dve.tensor_reduce(peak[:, 4:6], peak[:, 0:4].rearrange("h (i c) -> h i c", i=2), AX.X, ALU.max))
                step(own, dve.tensor_tensor(peak[:, 6:7], peak[:, 4:5], peak[:, 5:6], ALU.add))
                step(own, dve.tensor_scalar(above[0:HEADS, :], peak[:, 6:7], SAFE_SQUARES, None, ALU.is_gt))

            def before_tasks(n, turns, own, s):
                if s in AT_XN:
                    next_turn(turns)
                if s == AT_LN0:
                    dve.wait_ge(x_in, 16 * (n + 1))
                    layer_norm(own, X, st0, ln0, LN0_EPS, ln0_ready, deviation=True)
                if s in AT_Q + AT_K:
                    h = AT_Q.index(s) if s in AT_Q else AT_K.index(s)
                    if s == AT_Q[0]:
                        for j in range(PAIRS):
                            dve.wait_ge(stack_in[j], 32 + 16 * STACK_DMAS * n)
                    drain_a(turns)
                    drain_qk(own, A[:, :], s in AT_K, h).then_inc(a_drained, 1)
                if s in AT_V:
                    dve.wait_ge(va_ready, PAIRS * n)
                    drain_a(turns)
                    drain_v(A, AT_V.index(s)).then_inc(a_drained, 1)
                if s in AT_TOKX:
                    h = AT_TOKX.index(s)
                    dve.wait_ge(means_ready, n + 1)
                    drain_a(turns)
                    drain_tokx(A, h).then_inc(a_drained, 1)
                if s in AT_BOUND:
                    i = AT_BOUND.index(s)
                    drain_a(turns)
                    dve.tensor_reduce(peak[:, i:i + 1], A[0:HEADS, :], AX.X, ALU.max).then_inc(a_drained, 1)
                if s == AT_BOUND[3]:
                    dve.wait_ge(a_drained, turns[0] + turns[1])
                    bound(own)
                if s == AT_FLAG:
                    dve.wait_ge(mrow_in, 16 * HEADS * n)
                    drain_a(turns)
                    dve.tensor_copy(flag[:, :], A[0:1, 0:1]).then_inc(a_drained, 1)

            def row_maxima(n):
                for t in range(TILES):
                    for h in range(HEADS):
                        k = t * HEADS + h
                        dve.wait_ge(max_filled, MAX_TILES * n + k + 1)
                        dve.tensor_reduce(mx[:, h * TILES + t:h * TILES + t + 1], S[:, k % 2, :], AX.X, ALU.max)\
                            .then_inc(max_drained, 1)
                dve.wait_ge(max_turned, n + 1)
                dve.tensor_scalar(mneg[:, :], S[0:MAX_TILES, 0, 0:P], -1.0, None, ALU.mult).then_inc(mneg_ready, 1)

            def copy_o(n, j):
                dve.wait_ge(pv_done, STEPS * n + TILES * (j + 1))
                dve.tensor_copy(Ot[:, :], O[:, :]).then_inc(o_copied, 1)

            def divide_o(n, j, turns, own):
                drain_a(turns)
                o = A[:, :].rearrange("p (t a c e) -> p t a c e", t=4, a=2, c=2)
                r = rden[:, :].rearrange("p (t a c) -> p t a c", t=4, a=2)
                step(own, dve.reciprocal(rden[:, :].rearrange("p (u o) -> p u o", o=1),
                                        A[:, :].rearrange("p (u e) -> p u e", e=32)[:, :, HD:HD + 1]))
                for c in range(2):
                    ins = dve.tensor_tensor(
                        attn[:, 4 * c:4 * c + 4, 2 * HD * j:2 * HD * (j + 1)].rearrange("p t (a d) -> p t a d", a=2),
                        o[:, :, :, c, 0:HD], r[:, :, :, c:c + 1].to_broadcast([P, 4, 2, HD]), ALU.mult)
                ins.then_inc(a_drained, 1)

            def normal_form(own, src):
                layer_norm(own, src, st1, ln1, LN1_EPS, after_done)
                own[2] += 1
                dve.wait_ge(own[0], own[1] + own[2])
                for t in range(TILES):
                    ins = dve.tensor_scalar(that[:, t, :], src[:, t, :], ln1[:, 0, t:t + 1], ln1[:, 1, t:t + 1],
                                            ALU.subtract, ALU.mult)
                    if t % 4 == 3:
                        ins.then_inc(that_ready, 1)

            def after_tasks(n, own, s):
                if s == AT_AT:
                    for h in range(2):
                        bank, drained = drain_b(n, h)
                        dve.tensor_copy(half(attnT, h), bank[:, :]).then_inc(drained, 1)
                if s == AT_TOK:
                    dve.wait_ge(tokx_moved, n + 1)
                    for h in range(2):
                        bank, drained = drain_b(n, 2 + h)
                        dve.tensor_tensor(flat4(tok, h), bank[:, :], flat4(tokx, h), ALU.add).then_inc(drained, 1)
                        dve.wait_ge(drained, n * (AFTER // 2) + 2)
                    normal_form(own, tok)
                if s == AT_T:
                    for h in range(2):
                        dve.wait_ge(b_drained[h], n * (AFTER // 2) + 3)
                        fields = pooled[:, POS // 2 * h:POS // 2 * (h + 1)]
                        step(own, dve.tensor_reduce(fields.rearrange("p (y x) -> p y x", x=GRID),
                                                    half(tT, h).rearrange("p (y a x b) -> p y x a b", y=GRID // 2, a=POOL, x=GRID),
                                                    AX.XY, ALU.add))
                        dve.tensor_scalar(fields, fields, 1.0 / POOL ** 2, None, ALU.mult).then_inc(pooled_ready, 1)
                if s == AT_PK:
                    bank, drained = drain_b(n, 8)
                    keys = bank[0:ROWS1, 0:PAIRS * POS].rearrange("p (j k) -> p j k", j=PAIRS)

                    def place(rows1, part):
                        for a in range(2):
                            ins = dve.tensor_scalar(K1s[rows1, :, a, :], part[rows1, :, :].bitcast(fp32),
                                                    pair_mask[rows1, a:a + 1], None, ALU.mult)
                        return ins
                    low = slice(2 * HD, 4 * HD)
                    step(own, dve.tensor_copy(k1h[:, :, :], keys))
                    dve.tensor_tensor(k1l[low, :, :], keys[low, :, :], k1h[low, :, :].bitcast(fp32), ALU.subtract)
                    step(own, place(slice(0, ROWS1), k1h))
                    place(low, k1l).then_inc(drained, 1)
                    bank, drained = drain_b(n, 9)
                    dve.tensor_copy(pkv[:, :], bank[0:POS, 0:2 * C]).then_inc(drained, 1)
                for j in range(PAIRS):
                    if s != AT_SC[j]:
                        continue
                    for h in range(2):
                        k = 10 + 2 * j + h
                        bank, drained = drain_b(n, k)
                        ins = dve.tensor_reduce(r8[:, 2 * j + h:2 * j + h + 1], bank[:, :], AX.X, ALU.max)
                        if k < 17:
                            ins.then_inc(drained, 1)
                    if j == PAIRS - 1:
                        step(own, ins)
                        dve.tensor_reduce(r1[:, :], r8[:, :], AX.X, ALU.max).then_inc(b_drained[1], 1)
                if s == AT_RT:
                    bank, drained = drain_b(n, 18)
                    step(own, dve.tensor_copy(rrow[:, :], bank[0:1, 0:P]))
                    dve.tensor_tensor(red[:, :], rrow[:, 0:POS], rrow[:, POS:2 * POS], ALU.max).then_inc(drained, 1)
                if s == AT_RB:
                    bank, drained = drain_b(n, 19)
                    dve.tensor_copy(rB[:, :], bank[0:POS, 0:POS]).then_inc(drained, 1)
                    dve.wait_ge(drained, n * (AFTER // 2) + 10)
                    step(own, dve.tensor_tensor(rsel[:, :], rB[:, :], ident[0:POS, 0:POS], ALU.mult))
                    step(own, dve.tensor_reduce(rcol[:, :], rsel[:, :], AX.X, ALU.add))
                    dve.tensor_scalar(rgt[:, :], rB[:, :], rcol[:, 0:1], None, ALU.is_gt)
                    step(own, dve.scalar_tensor_tensor(out=rsel[:, :], in0=rB[:, :], scalar=rcol[:, 0:1], in1=below[:, :],
                                                      op0=ALU.is_equal, op1=ALU.mult))
                    step(own, dve.tensor_tensor(rgt[:, :], rgt[:, :], rsel[:, :], ALU.add))
                    step(own, dve.tensor_reduce(rank[:, :], rgt[:, :], AX.X, ALU.add))
                    dve.tensor_scalar(hot[:, :, :], iota_f[:, :].unsqueeze(1).to_broadcast([POS, HEADS, TOPK]),
                                      rank[:, 0:1], None, ALU.is_equal).then_inc(hot_ready, 1)
                if s == AT_SEL:
                    mask = head_mask[:, :].unsqueeze(2)
                    bank, drained = drain_b(n, 20)
                    dve.tensor_tensor(bd_k[:, :, :], bank[:, 0:TOPK].unsqueeze(1).to_broadcast([P, HEADS, TOPK]),
                                      mask.to_broadcast([P, HEADS, TOPK]), ALU.mult).then_inc(drained, 1)
                    bank, drained = drain_b(n, 21)
                    dve.tensor_tensor(bd_v[:, :, :], bank[:, 0:C].rearrange("p (h d) -> p h d", h=HEADS),
                                      mask.to_broadcast([P, HEADS, HD]), ALU.mult).then_inc(drained, 1)
                G = TILES * HEADS // 2
                if s == AT_S2:
                    for h in range(2):
                        bank, drained = drain_b(n, 22 + h)
                        sc = bank[:, :].rearrange("p (g k) -> p g k", k=TOPK)
                        step(own, dve.tensor_reduce(m2[:, G * h:G * h + G], sc, AX.X, ALU.max))
                        dve.tensor_tensor(E2[:, G * h:G * h + G, :], sc,
                                          m2[:, G * h:G * h + G].unsqueeze(2).to_broadcast([P, G, TOPK]),
                                          ALU.subtract).then_inc(drained, 1)
                if s == AT_E2:
                    for h in range(2):
                        g = slice(G * h, G * h + G)
                        dve.wait_ge(e2_exp, 2 * n + 1 + h)
                        step(own, dve.tensor_reduce(den2[:, g], E2[:, g, :], AX.X, ALU.add))
                        step(own, dve.reciprocal(m2[:, g], den2[:, g]))
                        dve.tensor_tensor(E2[:, g, :], E2[:, g, :], m2[:, g].unsqueeze(2).to_broadcast([P, G, TOPK]),
                                          ALU.mult).then_inc(e2_ready, 1)
                if s == AT_TOK2:
                    for h in range(2):
                        bank, drained = drain_b(n, 26 + h)
                        dve.tensor_tensor(flat4(tok2, h), bank[:, :], flat4(tok, h), ALU.add).then_inc(drained, 1)
                        dve.wait_ge(drained, n * (AFTER // 2) + 14)
                    normal_form(own, tok2)
                if s in AT_FF:
                    f = AT_FF.index(s)
                    for h in range(2):
                        bank, drained = drain_b(n, 32 + 2 * f + h)
                        dve.tensor_scalar(hT[:, f, h * HALF:(h + 1) * HALF], bank[:, :], cols[:, 8 + f:9 + f], None, ALU.add)\
                            .then_inc(drained, 1)
                if s in AT_OUT:
                    h = AT_OUT.index(s)
                    if h == 0 and not (isinstance(n, int) and n == 0):
                        dve.wait_ge(out_done, 2 * 16 * n)
                    bank, drained = drain_b(n, 36 + h)
                    dve.tensor_tensor(tiles4(Y, h), bank[:, :].rearrange("p (t c) -> p t c", t=4),
                                      out_bias[:, :].unsqueeze(1).to_broadcast([P, 4, C]), ALU.add).then_inc(drained, 1)

            dve.memset(all_ones[:, :], 1.0)
            dve.memset(ones_row[:, :], 1.0)
            dve.memset(ones_col[:, :], 1.0)
            dve.memset(above[:, :], 0.0)
            dve.memset(k_ones[:, :], 1.0).then_inc(vsetup, 1)
            dve.wait_ge(consts, 11)
            dve.tensor_copy(head_mask_b[:, :], head_mask[:, :])
            dve.tensor_copy(iota_f[:, :], iota_i[:, :]).then_inc(vsetup, 1)
            own = [first_steps, 0, 0]
            dve.wait_ge(x_in, 16)
            layer_norm(own, X, st0, ln0, LN0_EPS, ln0_ready, deviation=True)
            dve.wait_ge(ln0_ready, 1)
            for t in range(TILES):
                ins = dve.tensor_scalar(xn[:, t, :], X[:, t, :], ln0[:, 0, t:t + 1], ln0[:, 1, t:t + 1], ALU.subtract, ALU.mult)
                if t == 3:
                    ins.then_inc(half_xn, 1)
            ins.then_inc(xn_ready, 1)
            dve.wait_ge(qkv_in, 16 * QKV_DMAS)
            for i in range(4):
                hi, lo, bias = (kh, kl, BK) if i >= 2 else (qh, ql, BQ)
                dve.wait_ge(first_filled, 3 + i)
                dve.wait_ge(first_hi, 1 + i)
                dve.scalar_tensor_tensor(out=half(lo, i % 2), in0=FIRST[4 + i], scalar=bias, in1=half(hi, i % 2).bitcast(fp32),
                                         op0=ALU.add, op1=ALU.subtract).then_inc(first_dve, 1)
            for h in range(2):
                dve.wait_ge(first_filled, 7 + h)
                drain_v(FIRST[h], h).then_inc(first_dve, 1)
            dve.wait_ge(fold_in, 16 * FOLD_DMAS)
            dve.wait_ge(folded, 3)
            dve.tensor_tensor(tok_bias[:, :], BC[0][:, 0:C], rows[:, 1, :], ALU.add).then_inc(fold_added, 1)
            dve.tensor_tensor(out_bias[:, :], BC[0][:, C:2 * C], rows[:, 2, :], ALU.add).then_inc(fold_added, 1)
            dve.tensor_copy(win_sum[:, :], BC[0][:, 2 * C:3 * C]).then_inc(fold_added, 1)
            for i in range(4):
                dve.wait_ge(first_filled, 9 + i)
                dve.tensor_reduce(peak[:, i:i + 1], FIRST[4 + i][0:HEADS, :], AX.X, ALU.max).then_inc(first_dve, 1)
            dve.wait_ge(first_dve, 10)
            bound(own)
            assert own[2] == FIRST_STEPS
            dve.wait_ge(first_filled, 13)
            dve.tensor_copy(flag[:, :], FIRST[4][0:1, 0:1]).then_inc(first_dve, 1)
            dve.wait_ge(means_ready, 1)
            for h in range(2):
                dve.wait_ge(first_filled, 14 + h)
                drain_tokx(BC[h], h).then_inc(first_dve, 1)

            def image(n, base, first=False, last=False):
                wait_for_flag(dve, base)
                dve.sem_inc(dve_passed, 1)
                with dve.If(dve.value_load(flag[0:1, 0:1], min_val=0, max_val=HEADS) > 0):
                    row_maxima(n)
                with dve.Else():
                    dve.sem_inc(max_drained, MAX_TILES)
                    dve.sem_inc(mneg_ready, 1)
                turns = [base, 0]
                own_b = [before_done, n * BEFORE_STEPS, 0]
                own_a = [after_done, (n - 1) * AFTER_STEPS if not first else 0, 0]
                own_o = [att_done, n * PAIRS - (0 if first else 1), 0]
                for s in range(STEPS):
                    if s == 0 and not first:
                        copy_o(n - 1, PAIRS - 1)
                    if s > 0 and s % TILES == 0:
                        copy_o(n, s // TILES - 1)
                    if s == 1 and not first:
                        divide_o(n - 1, PAIRS - 1, turns, own_o)
                    if s > 1 and s % TILES == 1:
                        divide_o(n, s // TILES - 1, turns, own_o)
                    if not last:
                        before_tasks(n + 1, turns, own_b, s)
                    if not first:
                        after_tasks(n - 1, own_a, s)
                assert last or own_b[2] == BEFORE_STEPS
                assert first or own_a[2] == AFTER_STEPS

            image(0, 0, first=True)
            dve.wait_ge(weights_in, 16 * WEIGHT_DMAS)
            with dve.Fori(1, IMAGES - 1) as n:
                image(n, TURNS_0 + (n - 1) * TURNS)
            base = TURNS_0 + (IMAGES - 2) * TURNS
            image(IMAGES - 1, base, last=True)
            copy_o(IMAGES - 1, PAIRS - 1)
            divide_o(IMAGES - 1, PAIRS - 1, [base + PAIRS, 0], [att_done, IMAGES * PAIRS - 1, 0])
            own = [after_done, (IMAGES - 1) * AFTER_STEPS, 0]
            for s in range(STEPS):
                after_tasks(IMAGES - 1, own, s)


_INS = ['x', 'L0_conv_ln_scale', 'L0_conv_ln_bias', 'L0_conv_w_qkv', 'L0_conv_b_qkv', 'L0_conv_w_out', 'L0_conv_b_out',
        'L1_conv_Win', 'L1_conv_b_in', 'L1_conv_Wq', 'L1_conv_Wk', 'L1_conv_Wv', 'L1_conv_g1', 'L1_conv_be1',
        'L1_conv_g2', 'L1_conv_be2', 'L1_conv_Wf1', 'L1_conv_bf1', 'L1_conv_Wf2', 'L1_conv_bf2', 'L1_conv_Wout',
        'L1_conv_bout']
_OUTS = [((8, 32, 32, 128), 'float32')]


def kernel(**inputs):
    import numpy as _np
    import concourse.bacc as _bacc
    from concourse import mybir as _mybir
    from concourse.bass_utils import run_bass_kernel_spmd as _run

    nc = _bacc.Bacc("TRN2", target_bir_lowering=False, num_devices=1)
    arrays, args = {}, []
    for name in _INS:
        a = _np.ascontiguousarray(inputs[name])
        arrays[f"in_{name}_dram"] = a
        args.append(nc.dram_tensor(f"in_{name}_dram", a.shape, _mybir.dt.from_np(a.dtype), kind="ExternalInput").ap())
    for i, (shape, dtype) in enumerate(_OUTS):
        dt = _mybir.dt.from_np(_np.dtype(dtype))
        args.append(nc.dram_tensor(f"out_{i}_dram", shape, dt, kind="ExternalOutput").ap())
    two_layers(nc, *args)
    r = _run(nc, [arrays], core_ids=[0])
    got = tuple(r.results[0][f"out_{i}_dram"] for i in range(len(_OUTS)))
    return got[0]
```
